# Optimizing a Trainium2 kernel written in Bass

```python
import numpy as np
import jax
import jax.numpy as jnp

def _softmax(x, axis=-1):
    return jax.nn.softmax(x, axis=axis)

def _gelu(x):
    return jax.nn.gelu(x, approximate=True)

def _silu(x):
    return jax.nn.silu(x)

def _sigmoid(x):
    return jax.nn.sigmoid(x)

def _layernorm(x, axis=-1, eps=1e-05):
    m = jnp.mean(x, axis=axis, keepdims=True)
    v = jnp.var(x, axis=axis, keepdims=True)
    return (x - m) / jnp.sqrt(v + eps)

def _scatter_add(tgt, idx, src, axis=0):
    return tgt.at[idx].add(src)

def _segment_sum(src, seg, n):
    return jax.ops.segment_sum(src, seg, n)
kernel_name = 'mk_xattn_ffn_d1_seqx_r8_822f3d'

def setup_inputs(seed: int=0):
    np.random.seed(seed)
    _w = jnp.asarray

    def _rec_inputs():
        import jax
        import jax.numpy as jnp
        _rk = jax.random.key(seed)
        x = 0.0003765 + 1 * jax.random.normal(jax.random.fold_in(_rk, 1), (16, 128, 256), jnp.float32)
        _lenS = 128 - jax.random.randint(jax.random.fold_in(_rk, 7), (16,), 0, max(1, 128 // 4) + 1, jnp.int32)
        _lenS2 = 128 - jax.random.randint(jax.random.fold_in(_rk, 8), (16,), 0, max(1, 128 // 4) + 1, jnp.int32)
        _ctx_2048P = jax.random.normal(jax.random.fold_in(_rk, 11), (16, 16, 256), jnp.float32)
        _ctx_2048c = jax.random.dirichlet(jax.random.fold_in(_rk, 511), 0.3 * jnp.ones((16,), jnp.float32), (16, 128))
        _ctx_2048t = jnp.einsum('bsk,bkd->bsd', _ctx_2048c, _ctx_2048P)
        _ctx_2048t = _ctx_2048t * jax.lax.rsqrt(jnp.mean(jnp.square(_ctx_2048t)) + 1e-12) * 0.953939
        ctx_2048 = -0.000292821 + 1.00034 * (_ctx_2048t + 0.3 * jax.random.normal(jax.random.fold_in(_rk, 611), (16, 128, 256), jnp.float32))
        return (x, ctx_2048)
    x, ctx_2048 = _rec_inputs()

    def _L0_xattn_setup():
        import jax, jax.numpy as jnp
        import numpy as np
        key = jax.random.key(seed)
        k1, k2, k3, k4, k5 = jax.random.split(key, 5)
        B, D_MODEL, L = (2, 128, 256)
        HEAD_DIM = 8
        H = D_MODEL // HEAD_DIM
        return {'k': jax.random.normal(k1, (B, D_MODEL, L), dtype=jnp.float32), 'v': jax.random.normal(k2, (B, D_MODEL, L), dtype=jnp.float32), 'q': jax.random.normal(k3, (B, D_MODEL, L), dtype=jnp.float32), 'ssm_kernel': jax.random.normal(k4, (H, L), dtype=jnp.float32), 'D': jax.random.normal(k5, (H,), dtype=jnp.float32), 'head_dim': HEAD_DIM}
    _L0_xattn_all = _L0_xattn_setup()
    _L0_xattn_in = {k: v for k, v in _L0_xattn_all.items() if k in ('ssm_kernel', 'D')}
    del _L0_xattn_all

    def _L0_ffn_setup():
        import jax, jax.numpy as jnp
        import numpy as np
        B, S, H = (4, 512, 256)
        E, I, TOP_K = (8, 128, 2)
        key = jax.random.key(seed)
        ks = jax.random.split(key, 6)
        sc = 0.02
        return {'x': jax.random.normal(ks[0], (B, S, H), dtype=jnp.float32), 'w_gate': jax.random.normal(ks[1], (H, E), dtype=jnp.float32) * sc, 'W1': jax.random.normal(ks[2], (E, H, I), dtype=jnp.float32) * sc, 'b1': jnp.zeros((E, I), dtype=jnp.float32), 'W2': jax.random.normal(ks[3], (E, I, H), dtype=jnp.float32) * sc, 'b2': jnp.zeros((E, H), dtype=jnp.float32)}
    _L0_ffn_all = _L0_ffn_setup()
    _L0_ffn_in = {k: v for k, v in _L0_ffn_all.items() if k in ('w_gate', 'W1', 'b1', 'W2', 'b2')}
    del _L0_ffn_all
    return {'x': x, 'ctx_2048': ctx_2048, 'L0_xattn_ssm_kernel': _L0_xattn_in['ssm_kernel'], 'L0_xattn_D': _L0_xattn_in['D'], 'L0_ffn_w_gate': _L0_ffn_in['w_gate'], 'L0_ffn_W1': _L0_ffn_in['W1'], 'L0_ffn_b1': _L0_ffn_in['b1'], 'L0_ffn_W2': _L0_ffn_in['W2'], 'L0_ffn_b2': _L0_ffn_in['b2']}

def reference(x, ctx_2048, L0_xattn_ssm_kernel, L0_xattn_D, L0_ffn_w_gate, L0_ffn_W1, L0_ffn_b1, L0_ffn_W2, L0_ffn_b2):
    import jax
    import jax.numpy as jnp

    def _L0_xattn_ref(k, v, q, ssm_kernel, D, head_dim):
        import jax, jax.numpy as jnp
        import numpy as np
        B, HD, L = k.shape
        H = HD // head_dim
        fft_size = 2 * L
        k_ = k.reshape(B, H, head_dim, L)
        v_ = v.reshape(B, H, head_dim, L)
        q_ = q.reshape(B, H, head_dim, L)
        kv = jnp.einsum('bhil,bhjl->bijhl', k_, v_)
        kv_f = jnp.fft.rfft(kv, n=fft_size)
        kernel_f = jnp.fft.rfft(ssm_kernel, n=fft_size)
        y = jnp.fft.irfft(kv_f * kernel_f, n=fft_size)[..., :L]
        out = y + kv * D[None, None, None, :, None]
        out = jnp.einsum('bijhl,bhil->bjhl', out, q_)
        out = jnp.transpose(out, (0, 2, 1, 3)).reshape(B, H * head_dim, L)
        return out.astype(k.dtype)

    def _L0_ffn_ref(x, w_gate, W1, b1, W2, b2):
        import jax, jax.numpy as jnp
        import numpy as np
        B, S, H = (4, 512, 256)
        E, I, TOP_K = (8, 128, 2)
        Bm, Sm, Hm = x.shape
        x_flat = x.reshape(-1, Hm)
        gate_logits = x_flat @ w_gate
        raw_weights = jax.nn.softmax(gate_logits, axis=-1)
        topk_w, topk_idx = jax.lax.top_k(raw_weights, TOP_K)
        topk_w = jax.nn.softmax(topk_w, axis=-1)
        combine = jnp.sum(jax.nn.one_hot(topk_idx, E, dtype=x.dtype) * topk_w[..., None], axis=1)
        out = jnp.zeros_like(x_flat)
        for e in range(E):
            h = jax.nn.gelu(x_flat @ W1[e] + b1[e], approximate=False)
            y = h @ W2[e] + b2[e]
            out = out + combine[:, e:e + 1] * y
        return out.reshape(Bm, Sm, Hm)
    x = x + _L0_xattn_ref(ctx_2048, ctx_2048, _layernorm(x, axis=-1), L0_xattn_ssm_kernel, L0_xattn_D, 8)
    x = x + _L0_ffn_ref(_layernorm(x, axis=-1), L0_ffn_w_gate, L0_ffn_W1, L0_ffn_b1, L0_ffn_W2, L0_ffn_b2)
    return x

_drawn_inputs = setup_inputs


def setup_inputs(seed=0):
    import zlib

    import numpy as np

    out = dict(_drawn_inputs(seed))
    spreads = {'L0_ffn_b1': (0.0, 2.0), 'L0_ffn_b2': (0.0, 2.0)}
    factors = {'L0_ffn_w_gate': 8.0, 'L0_ffn_W1': 8.0, 'L0_ffn_W2': 8.0}
    for name, (base, spread) in spreads.items():
        noise = np.random.default_rng([zlib.crc32(name.encode()), seed]).standard_normal(out[name].shape)
        drawn = base * np.exp(spread * noise) if base else spread * noise
        out[name] = jnp.asarray(drawn.astype(out[name].dtype))
    for name, factor in factors.items():
        out[name] = (out[name] * factor).astype(out[name].dtype)
    return out
```

```python
from contextlib import ExitStack

import concourse.bass as bass
from concourse import mybir

B, HD, L = 16, 128, 256
H, DH = 16, 8
E, I = 8, 128
P = 128
GB = 4
G = B // GB
NC = L // P
CB = NC * GB
TOK = GB * P
ND = DH // 2 + 1
NPAIR = ND * DH
W = DH + ND - 1
HS = 2
STEPS = H // HS
ZW = 72
EPS = 1e-5
EULER = 2.718281828459045


def block_kernel(nc, x, ctx_in, toep_src, d_src, wgate, w1, b1t, w2, b2, out):
    F32 = mybir.dt.float32
    F32R = mybir.dt.float32r
    ALU = mybir.AluOpType
    ACT = mybir.ActivationFunctionType
    AX = mybir.AxisListType.X

    ctx = ExitStack()
    with ctx:
        def sb(name, shape, dt=F32):
            return ctx.enter_context(nc.sbuf_tensor(name, shape, dt))

        def pb(name):
            return ctx.enter_context(nc.psum_tensor(name, [P, 512], F32))

        def sem(name):
            return ctx.enter_context(nc.semaphore(name))

        toep = sb("toep", [P, H, L])
        w1_sb = sb("w1_sb", [P, NC, E, I])
        w2_sb = sb("w2_sb", [P, E, L])
        wg_sb = sb("wg_sb", [P, NC, E])
        b1_sb = sb("b1_sb", [P, E])
        b2_sb = sb("b2_sb", [2 * E, L])
        b2hi = sb("b2hi", [2 * E, L], F32R)
        b2lo = sb("b2lo", [2 * E, L], F32R)
        d_sb = sb("d_sb", [P, H])
        ident = sb("ident", [P, P])
        ones = sb("ones", [P, P])
        rank_sb = sb("rank_sb", [P, GB, E])
        half = sb("half", [P, GB])
        euler = sb("euler", [P, GB, E])
        pick = sb("pick", [2 * E, E, P])
        pickr = sb("pickr", [2 * E, E, P], F32R)
        x_sb = sb("x_sb", [P, B, L])
        ctx_sb = sb("ctx_sb", [P, GB, L])
        xn = sb("xn", [P, GB, L])
        kx = sb("kx", [P, H, NC, GB, W])
        qx = sb("qx", [P, H, NC, GB, W])
        kv = sb("kv", [P, 2, HS, CB * NPAIR])
        z = sb("z", [P, 2, HS, CB, ZW])
        o_sb = sb("o_sb", [P, CB, HD])
        st1 = sb("st1", [P, GB, 6])
        mo1 = sb("mo1", [P, 7, GB])
        rs1 = sb("rs1", [P, GB])
        st2 = sb("st2", [P, GB, 6])
        mo2 = sb("mo2", [P, 7, GB])
        rs2 = sb("rs2", [P, GB])
        xn2 = sb("xn2", [P, GB, L])
        xT = sb("xT", [P, NC, TOK])
        lmax = sb("lmax", [P, GB])
        lsub = sb("lsub", [P, GB, E])
        lexp = sb("lexp", [P, GB, E])
        lsum = sb("lsum", [P, GB])
        lrec = sb("lrec", [P, GB])
        raw = sb("raw", [P, GB, E])
        raw2 = sb("raw2", [P, GB, E])
        top = sb("top", [P, 2, GB])
        eq = sb("eq", [P, GB, E])
        eqr = sb("eqr", [P, GB, E])
        first = sb("first", [P, GB])
        tdif = sb("tdif", [P, GB])
        texp = sb("texp", [P, GB])
        tden = sb("tden", [P, GB])
        tw = sb("tw", [P, GB, 2])
        oh1 = sb("oh1", [P, GB, E])
        oh2 = sb("oh2", [P, GB, E])
        oh1w = sb("oh1w", [P, GB, E])
        oh2w = sb("oh2w", [P, GB, E])
        comb = sb("comb", [P, GB, E])
        combh = sb("combh", [P, GB, E], F32R)
        comb2 = sb("comb2", [P, GB, 2 * E])
        cT = sb("cT", [2 * E, TOK], F32R)
        hg = sb("hg", [P, 2, TOK])
        hc = sb("hc", [P, E, TOK])

        y_ps = [pb(f"y_ps{i}") for i in range(2)]
        m1_ps = [pb(f"m1_ps{i}") for i in range(2)]
        ob_ps = [pb(f"ob_ps{i}") for i in range(2)]
        tr_ps = [pb(f"tr_ps{i}") for i in range(2)]

        x0_in = sem("x0_in")
        x_in = sem("x_in")
        c_in = sem("c_in")
        toep_in = [sem(f"toep_in{i}") for i in range(4)]
        d_in = sem("d_in")
        w_in = sem("w_in")
        stored = sem("stored")
        fill_ok = sem("fill_ok")
        consts = sem("consts")
        toep_mul = sem("toep_mul")
        toep_ok = sem("toep_ok")
        b2_ok = sem("b2_ok")
        pick_ok = sem("pick_ok")
        ctxT_ps = sem("ctxT_ps")
        kx_ok = sem("kx_ok")
        kxw_ok = sem("kxw_ok")
        moments1 = sem("moments1")
        rstd1 = sem("rstd1")
        xn_ok = sem("xn_ok")
        xnT_ps = sem("xnT_ps")
        qx_ok = sem("qx_ok")
        kv_ok = sem("kv_ok")
        y_ok = sem("y_ok")
        z_ok = sem("z_ok")
        fold1 = sem("fold1")
        fold2 = sem("fold2")
        fold3 = sem("fold3")
        o_ok = sem("o_ok")
        oT_ps = sem("oT_ps")
        x2_ok = sem("x2_ok")
        moments2 = sem("moments2")
        rstd2 = sem("rstd2")
        xn2_ok = sem("xn2_ok")
        x2T_ps = sem("x2T_ps")
        xT_ok = sem("xT_ok")
        logit_ps = sem("logit_ps")
        route = sem("route")
        lexp_ok = sem("lexp_ok")
        texp_ok = sem("texp_ok")
        cT_ps = sem("cT_ps")
        cT_ok = sem("cT_ok")
        m1_ok = sem("m1_ok")
        gelu_ok = sem("gelu_ok")
        cb_ok = sem("cb_ok")
        hc_ok = sem("hc_ok")
        m2_ok = sem("m2_ok")
        out_ok = sem("out_ok")
        MOMENTS = 5
        ROUTE = 26

        def after(eng, s, value):
            if not isinstance(value, int) or value > 0:
                eng.wait_ge(s, value)

        def batches(g, first, n):
            return bass.ds(g * GB + first, n)

        toep_rows = H // len(toep_in)
        block = ctx.enter_context(nc.Block())

        @block.sync
        def _(sp):
            def load_ctx(g):
                sp.dma_start(ctx_sb[:], ctx_in[batches(g, 0, GB)].rearrange("b p l -> p b l")).then_inc(c_in, 16)

            def store(n):
                for t in range(GB):
                    sp.wait_ge(out_ok, n * GB + t + 1)
                    sp.dma_start(out[batches(n, t, 1)].rearrange("b p l -> p b l"),
                                 x_sb[:, batches(n, t, 1), :]).then_inc(stored, 16)

            load_ctx(0)
            sp.dma_start(x_sb[:, 0:GB, :], x[0:GB].rearrange("b p l -> p b l")).then_inc(x0_in, 16)
            sp.dma_start(d_sb[:], d_src).then_inc(d_in, 16)
            for i, s in enumerate(toep_in):
                h0 = i * toep_rows
                sp.dma_start(toep[:, h0:h0 + toep_rows, :], toep_src[:, h0:h0 + toep_rows, :]).then_inc(s, 16)
            sp.dma_start(x_sb[:, GB:B, :], x[GB:B].rearrange("b p l -> p b l")).then_inc(x_in, 16)
            for c in range(NC):
                sp.dma_start(w1_sb[:, c], w1[:, c * P:(c + 1) * P].rearrange("e p i -> p e i")).then_inc(w_in, 16)
            sp.dma_start(w2_sb[:], w2.rearrange("e i l -> i e l")).then_inc(w_in, 16)
            sp.dma_start(wg_sb[:], wgate.rearrange("(c p) e -> p c e", p=P)).then_inc(w_in, 16)
            sp.dma_start(b1_sb[:], b1t).then_inc(w_in, 16)
            sp.dma_start(b2_sb[0:E, :], b2).then_inc(w_in, 16)
            sp.dma_start(b2_sb[E:2 * E, :], b2).then_inc(w_in, 16)
            sp.wait_ge(ctxT_ps, NC)
            load_ctx(1)
            with nc.sync.Fori(1, G - 1) as g:
                sp.wait_ge(ctxT_ps, (g + 1) * NC)
                load_ctx(g + 1)
                store(g - 1)
            store(G - 2)
            store(G - 1)
            sp.wait_ge(stored, 16 * B)

        WEIGHTS = 7 * 16

        @block.tensor
        def _(pe):
            def inputs_T(n):
                pe.wait_ge(c_in, (n + 1) * 16)
                after(pe, route, (n - 1) * ROUTE)
                after(pe, cT_ok, n - 1)
                for c in range(NC):
                    for b in range(GB):
                        t = nc.tensor.transpose(tr_ps[c][:, b * P:(b + 1) * P],
                                                ctx_sb[:, b, c * P:(c + 1) * P], ident[:])
                    t.then_inc(ctxT_ps, 1)
                pe.wait_ge(xn_ok, (n + 1) * GB)
                for c in range(NC):
                    pe.wait_ge(kxw_ok, n * NC + c + 1)
                    for b in range(GB):
                        t = nc.tensor.transpose(tr_ps[c][:, b * P:(b + 1) * P],
                                                xn[:, b, c * P:(c + 1) * P], ident[:])
                    t.then_inc(xnT_ps, 1)

            def convolve(g, s, first):
                pe.wait_ge(kv_ok, g * STEPS + s + 1)
                for hh in range(HS):
                    h = s * HS + hh
                    if first and h % toep_rows == 0:
                        pe.wait_ge(toep_ok, h // toep_rows + 1)
                    after(pe, z_ok, g * H + h - 1)
                    yp, k = y_ps[h % 2], kv[:, s % 2, hh, :]
                    n = GB * NPAIR
                    nc.tensor.matmul(yp[:, 0:2 * n], toep[:, h, 0:P], k, start=True, stop=False)
                    nc.tensor.matmul(yp[:, n:2 * n], toep[:, h, P:2 * P], k[:, 0:n],
                                     start=False, stop=True).then_inc(y_ok, 1)

            def up(n, e):
                if e == 0:
                    pe.wait_ge(xT_ok, (n + 1) * NC)
                after(pe, gelu_ok, n * E + max(e - 1, 0))
                for c in range(NC):
                    t = nc.tensor.matmul(m1_ps[e % 2][:], w1_sb[:, c, e, :], xT[:, c, :],
                                         start=(c == 0), stop=(c == NC - 1))
                t.then_inc(m1_ok, 1)

            def combine_T(n):
                pe.wait_ge(route, (n + 1) * ROUTE)
                for t in range(GB):
                    last = nc.tensor.transpose(tr_ps[1][0:2 * E, t * P:(t + 1) * P], comb2[:, t, :], ident[:])
                last.then_inc(cT_ps, 1)

            def spread(n, e):
                if e == 0:
                    pe.wait_ge(cT_ok, n + 1)
                if e < 2:
                    after(pe, out_ok, n * GB)
                else:
                    pe.wait_ge(hc_ok, n * E + e - 1)
                nc.tensor.matmul(ob_ps[e % 2][:], pickr[:, e, :], cT[:], start=True, stop=True).then_inc(cb_ok, 1)

            def down(n, t):
                if t == 0:
                    pe.wait_ge(hc_ok, (n + 1) * E)
                else:
                    after(pe, out_ok, n * GB + t - 1)
                o = ob_ps[t % 2][:, 0:L]
                tok = slice(t * P, (t + 1) * P)
                for e in range(E):
                    nc.tensor.matmul(o, hc[:, e, tok], w2_sb[:, e, :], start=(e == 0), stop=False)
                nc.tensor.matmul(o, cT[:, tok], b2hi[:], start=False, stop=False)
                nc.tensor.matmul(o, cT[:, tok], b2lo[:], start=False, stop=True).then_inc(m2_ok, 1)

            def attention_T(g, last):
                pe.wait_ge(o_ok, (g + 1) * STEPS)
                for p in range(2):
                    pe.wait_ge(qx_ok, ((g + 1) if last else (g + 2)) * NC)
                    for bb in range(2):
                        for c in range(NC):
                            t = nc.tensor.transpose(tr_ps[p][:, bb * L + c * P:bb * L + (c + 1) * P],
                                                    o_sb[:, c * GB + 2 * p + bb, :], ident[:])
                    t.then_inc(oT_ps, 1)

            def normed_T(g):
                pe.wait_ge(xn2_ok, (g + 1) * GB)
                for c in range(NC):
                    for b in range(GB):
                        t = nc.tensor.transpose(tr_ps[c][:, b * P:(b + 1) * P],
                                                xn2[:, b, c * P:(c + 1) * P], ident[:])
                    t.then_inc(x2T_ps, 1)

            def logits(g):
                pe.wait_ge(xT_ok, (g + 1) * NC)
                for t in range(GB):
                    for c in range(NC):
                        m = nc.tensor.matmul(tr_ps[0][:, t * E:(t + 1) * E], xT[:, c, t * P:(t + 1) * P],
                                             wg_sb[:, c, :], start=(c == 0), stop=(c == NC - 1))
                m.then_inc(logit_ps, 1)

            def experts_up(n, s):
                if s == 0:
                    up(n, 0)
                    combine_T(n)
                else:
                    up(n, s)
                    spread(n, s - 1)

            def iteration(g, last):
                for s in range(STEPS):
                    convolve(g, s, False)
                    experts_up(g - 1, s)
                spread(g - 1, E - 1)
                down(g - 1, 0)
                if not last:
                    inputs_T(g + 1)
                down(g - 1, 1)
                attention_T(g, last)
                down(g - 1, 2)
                normed_T(g)
                down(g - 1, 3)
                logits(g)

            pe.wait_ge(consts, 1)
            inputs_T(0)
            for s in range(STEPS):
                convolve(0, s, True)
            inputs_T(1)
            attention_T(0, False)
            normed_T(0)
            pe.wait_ge(w_in, WEIGHTS)
            logits(0)
            pe.wait_ge(pick_ok, 1)
            pe.wait_ge(b2_ok, 2)
            with nc.tensor.Fori(1, G - 1) as g:
                iteration(g, False)
            iteration(G - 1, True)
            for s in range(STEPS):
                experts_up(G - 1, s)
            spread(G - 1, E - 1)
            for t in range(GB):
                down(G - 1, t)

        @block.scalar
        def _(act):
            def widen(dst, c):
                src = tr_ps[c][:].rearrange("p (b h i) -> p b h i", b=GB, h=H)
                d = dst[:, :, c, :, :].rearrange("p h b w -> p b h w")
                nc.scalar.copy(d[:, :, :, 0:DH], src)
                return nc.scalar.copy(d[:, :, :, DH:W], src[:, :, :, 0:W - DH])

            def inputs(n):
                after(act, kv_ok, n * STEPS)
                for c in range(NC):
                    act.wait_ge(ctxT_ps, n * NC + c + 1)
                    widen(kx, c).then_inc(kxw_ok, 1)
                after(act, z_ok, n * H)
                for c in range(NC):
                    act.wait_ge(xnT_ps, n * NC + c + 1)
                    widen(qx, c).then_inc(qx_ok, 1)

            def normed(g):
                after(act, m1_ok, g * E)
                for c in range(NC):
                    act.wait_ge(x2T_ps, g * NC + c + 1)
                    nc.scalar.copy(xT[:, c, :], tr_ps[c][:]).then_inc(xT_ok, 1)

            def gelu(n, e):
                act.wait_ge(m1_ok, n * E + e + 1)
                after(act, hc_ok, n * E + max(e - 1, 0))
                nc.scalar.activation(hg[:, e % 2, :], m1_ps[e % 2][:], ACT.Gelu,
                                     bias=b1_sb[:, e:e + 1], scale=1.0).then_inc(gelu_ok, 1)

            inputs(0)
            inputs(1)
            normed(0)
            act.wait_ge(w_in, WEIGHTS)
            with nc.scalar.Fori(1, G - 1) as g:
                for e in range(E):
                    gelu(g - 1, e)
                inputs(g + 1)
                normed(g)
            for e in range(E):
                gelu(G - 2, e)
            normed(G - 1)
            for e in range(E):
                gelu(G - 1, e)

        @block.vector
        def _(dve):
            def norm(g, src, st, mo, rs, dst, marks, free):
                done_, rstd_, norm_ = marks
                k = [0]

                def step(ins):
                    k[0] += 1
                    ins.then_inc(done_, 1)
                    if k[0] < MOMENTS:
                        dve.wait_ge(done_, g * MOMENTS + k[0])

                for b in range(GB):
                    last = nc.vector.bn_stats(st[:, b, :], src(b))
                step(last)
                nc.vector.tensor_tensor(mo[:, 0], st[:, :, 1], st[:, :, 4], ALU.add)
                nc.vector.tensor_tensor(mo[:, 1], st[:, :, 1], st[:, :, 4], ALU.subtract)
                step(nc.vector.tensor_tensor(mo[:, 2], st[:, :, 2], st[:, :, 5], ALU.add))
                nc.vector.tensor_scalar(mo[:, 3], mo[:, 0], 0.5, None, ALU.mult)
                step(nc.vector.scalar_tensor_tensor(mo[:, 4], mo[:, 1], L / 4, mo[:, 1], ALU.mult, ALU.mult))
                step(nc.vector.tensor_tensor(mo[:, 5], mo[:, 4], mo[:, 2], ALU.add))
                step(nc.vector.tensor_scalar(mo[:, 6], mo[:, 5], 1 / L, EPS, ALU.mult, ALU.add))
                assert k[0] == MOMENTS
                yield
                dve.wait_ge(rstd_, g + 1)
                free()
                for b in range(GB):
                    nc.vector.tensor_scalar(dst[:, b, :], src(b), mo[:, 3, b:b + 1], rs[:, b:b + 1],
                                            ALU.subtract, ALU.mult).then_inc(norm_, 1)
                yield

            def norm1(n):
                return norm(n, lambda b: x_sb[:, batches(n, b, 1), :].rearrange("p b l -> p (b l)"),
                            st1, mo1, rs1, xn, (moments1, rstd1, xn_ok),
                            lambda: after(dve, xnT_ps, n * NC))

            def norm2(g):
                return norm(g, lambda b: x_sb[:, batches(g, b, 1), :].rearrange("p b l -> p (b l)"),
                            st2, mo2, rs2, xn2, (moments2, rstd2, xn2_ok),
                            lambda: after(dve, x2T_ps, g * NC))

            def times_q(g, s):
                if s == 0:
                    dve.wait_ge(qx_ok, (g + 1) * NC)
                after(dve, o_ok, g * STEPS + s - 1)
                for hh in range(HS):
                    h = s * HS + hh
                    dve.wait_ge(y_ok, g * H + h + 1)
                    yv = y_ps[h % 2][:, 0:CB * NPAIR].rearrange("p (c d i) -> p c d i", c=CB, d=ND)
                    q = qx[:, h, :, :, :].rearrange("p c b w -> p (c b) w")
                    q_far = bass.AP(tensor=q.tensor, offset=q.offset, ap=[*q.ap[:2], [1, ND], [1, DH]])
                    rows = z[:, s % 2, hh, :, :]
                    nc.vector.tensor_tensor(rows[:, :, 0:NPAIR].rearrange("p c (d i) -> p c d i", d=ND),
                                            yv, q_far, ALU.mult)
                    q_near = bass.AP(tensor=q.tensor, offset=q.offset, ap=[*q.ap[:2], [0, ND - 2], [1, DH]])
                    lo = NPAIR + 1
                    mirror = rows[:, :, lo:lo + (ND - 2) * (DH + 1)].rearrange(
                        "p c (d i) -> p c d i", d=ND - 2)[:, :, :, 0:DH]
                    nc.vector.tensor_tensor(mirror, yv[:, :, 1:ND - 1, :], q_near, ALU.mult).then_inc(z_ok, 1)

            def fold(g, s):
                dve.wait_ge(z_ok, g * H + (s + 1) * HS)
                zz = z[:, s % 2].rearrange("p h c w -> p (h c) w")
                nc.vector.tensor_tensor(zz[:, :, 0:32], zz[:, :, 0:32], zz[:, :, 32:64], ALU.add).then_inc(fold1, 1)

            def residual(g):
                for p in range(2):
                    dve.wait_ge(oT_ps, g * 2 + p + 1)
                    xs = x_sb[:, batches(g, 2 * p, 2), :]
                    nc.vector.tensor_tensor(xs, xs, tr_ps[p][:].rearrange("p (b l) -> p b l", b=2),
                                            ALU.add).then_inc(x2_ok, 1)

            def router(n):
                k = [0]

                def step(ins):
                    k[0] += 1
                    ins.then_inc(route, 1)
                    dve.wait_ge(route, n * ROUTE + k[0])

                def wide(ap):
                    return bass.AP(tensor=ap.tensor, offset=ap.offset, ap=[*ap.ap[:2], [0, E]])

                rank = rank_sb[:, :, :]
                lg = tr_ps[0][:, 0:GB * E].rearrange("p (t e) -> p t e", t=GB)
                dve.wait_ge(logit_ps, n + 1)
                step(nc.vector.reduce_max(lmax[:], lg, AX))
                step(nc.vector.tensor_tensor(lsub[:], lg, wide(lmax[:]), ALU.subtract))
                dve.wait_ge(lexp_ok, n + 1)
                step(nc.vector.reduce_sum(lsum[:], lexp[:], AX))
                step(nc.vector.reciprocal(lrec[:], lsum[:]))
                step(nc.vector.tensor_tensor(raw[:], lexp[:], wide(lrec[:]), ALU.mult))
                step(nc.vector.reduce_max(top[:, 0], raw[:], AX))
                step(nc.vector.tensor_tensor(eq[:], raw[:], wide(top[:, 0]), ALU.is_equal))
                step(nc.vector.tensor_tensor(eqr[:], eq[:], rank, ALU.mult))
                step(nc.vector.reduce_max(first[:], eqr[:], AX))
                step(nc.vector.tensor_tensor(oh1[:], rank, wide(first[:]), ALU.is_equal))
                step(nc.vector.scalar_tensor_tensor(raw2[:], oh1[:], -2.0, raw[:], ALU.mult, ALU.add))
                step(nc.vector.reduce_max(top[:, 1], raw2[:], AX))
                step(nc.vector.tensor_tensor(tdif[:], top[:, 1], top[:, 0], ALU.subtract))
                step(nc.vector.tensor_tensor(eq[:], raw2[:], wide(top[:, 1]), ALU.is_equal))
                step(nc.vector.tensor_tensor(eqr[:], eq[:], rank, ALU.mult))
                step(nc.vector.reduce_max(first[:], eqr[:], AX))
                step(nc.vector.tensor_tensor(oh2[:], rank, wide(first[:]), ALU.is_equal))
                dve.wait_ge(texp_ok, n + 1)
                step(nc.vector.tensor_scalar(tden[:], texp[:], 1.0, None, ALU.add))
                step(nc.vector.reciprocal(tw[:, :, 0], tden[:]))
                step(nc.vector.tensor_tensor(tw[:, :, 1], texp[:], tw[:, :, 0], ALU.mult))
                step(nc.vector.tensor_tensor(oh1w[:], oh1[:], wide(tw[:, :, 0]), ALU.mult))
                step(nc.vector.tensor_tensor(oh2w[:], oh2[:], wide(tw[:, :, 1]), ALU.mult))
                step(nc.vector.tensor_tensor(comb[:], oh1w[:], oh2w[:], ALU.add))
                step(nc.vector.tensor_copy(combh[:], comb[:]))
                after(dve, cT_ps, n)
                step(nc.vector.tensor_copy(comb2[:, :, 0:E], combh[:].bitcast(F32)))
                step(nc.vector.tensor_tensor(comb2[:, :, E:2 * E], comb[:], combh[:].bitcast(F32), ALU.subtract))
                assert k[0] == ROUTE

            def combine(n):
                dve.wait_ge(cT_ps, n + 1)
                after(dve, m2_ok, n * GB)
                nc.vector.tensor_copy(cT[:], tr_ps[1][0:2 * E, :]).then_inc(cT_ok, 1)

            def weigh(n, e):
                dve.wait_ge(gelu_ok, n * E + e + 1)
                dve.wait_ge(cb_ok, n * E + e + 1)
                if e == 0:
                    after(dve, m2_ok, n * GB)
                nc.vector.tensor_tensor(hc[:, e, :], hg[:, e % 2, :], ob_ps[e % 2][:], ALU.mult).then_inc(hc_ok, 1)

            def finish(n, t):
                dve.wait_ge(m2_ok, n * GB + t + 1)
                xs = x_sb[:, batches(n, t, 1), :].rearrange("p b l -> p (b l)")
                nc.vector.tensor_tensor(xs, xs, ob_ps[t % 2][:, 0:L], ALU.add).then_inc(out_ok, 1)

            def iteration(g, last):
                router(g - 1)
                n1 = None if last else norm1(g + 1)
                for s in range(STEPS):
                    times_q(g, s)
                    fold(g, s)
                    if s == 0:
                        combine(g - 1)
                    else:
                        weigh(g - 1, s - 1)
                    if n1 and s in (2, 4):
                        next(n1)
                weigh(g - 1, E - 1)
                finish(g - 1, 0)
                residual(g)
                dve.wait_ge(x2_ok, (g + 1) * 2)
                finish(g - 1, 1)
                n2 = norm2(g)
                next(n2)
                finish(g - 1, 2)
                next(n2)
                finish(g - 1, 3)

            dve.wait_ge(x0_in, 16)
            n1 = norm1(0)
            next(n1)
            next(n1)
            dve.wait_ge(consts, 1)
            dve.wait_ge(d_in, 16)
            idb = bass.AP(tensor=ident.tensor if hasattr(ident, "tensor") else ident,
                          offset=0, ap=[[P, P], [0, H], [1, P]])
            diag = hc[:, 0:H * P // TOK, :].rearrange("p e (h l) -> p (e h) l", l=P)
            dwide = bass.AP(tensor=d_sb.tensor if hasattr(d_sb, "tensor") else d_sb,
                            offset=0, ap=[[H, P], [1, H], [0, P]])
            nc.vector.tensor_tensor(diag, idb, dwide, ALU.mult).then_inc(toep_mul, 1)
            dve.wait_ge(toep_mul, 1)
            for i, s in enumerate(toep_in):
                dve.wait_ge(s, 16)
                hs = slice(i * toep_rows, (i + 1) * toep_rows)
                nc.vector.tensor_tensor(toep[:, hs, 0:P], toep[:, hs, 0:P], diag[:, hs, :],
                                        ALU.add).then_inc(toep_ok, 1)
            dve.wait_ge(x_in, 16)
            dve.wait_ge(consts, 2)
            n1 = norm1(1)
            for s in range(STEPS):
                times_q(0, s)
                fold(0, s)
                if s in (2, 4):
                    next(n1)
            residual(0)
            n2 = norm2(0)
            dve.wait_ge(x2_ok, 2)
            next(n2)
            dve.wait_ge(w_in, WEIGHTS)
            nc.vector.tensor_copy(b2hi[:], b2_sb[:]).then_inc(b2_ok, 1)
            nc.vector.tensor_copy(pickr[:], pick[:]).then_inc(pick_ok, 1)
            dve.wait_ge(b2_ok, 1)
            nc.vector.tensor_tensor(b2lo[:], b2_sb[:], b2hi[:].bitcast(F32), ALU.subtract).then_inc(b2_ok, 1)
            next(n2)
            with nc.vector.Fori(1, G - 1) as g:
                iteration(g, False)
            iteration(G - 1, True)
            router(G - 1)
            combine(G - 1)
            for e in range(E):
                weigh(G - 1, e)
            for t in range(GB):
                finish(G - 1, t)

        @block.gpsimd
        def _(pool):
            def rstd(g, mo, rs, moments, rstd_):
                pool.wait_ge(moments, (g + 1) * MOMENTS)
                nc.gpsimd.tensor_tensor(rs[:], mo[:, 6], half[:], ALU.pow).then_inc(rstd_, 1)

            def rstd_1(n):
                rstd(n, mo1, rs1, moments1, rstd1)

            def rstd_2(g):
                rstd(g, mo2, rs2, moments2, rstd2)

            def pairs(g, s):
                if s == 0:
                    pool.wait_ge(kxw_ok, (g + 1) * NC)
                after(pool, y_ok, g * H + (s - 1) * HS)
                k = kx[:, s * HS:(s + 1) * HS].rearrange("p h c b w -> p (h c b) w")
                near = bass.AP(tensor=k.tensor, offset=k.offset, ap=[*k.ap[:2], [0, ND], [1, DH]])
                far = bass.AP(tensor=k.tensor, offset=k.offset, ap=[*k.ap[:2], [1, ND], [1, DH]])
                dst = kv[:, s % 2].rearrange("p h (c d i) -> p (h c) d i", d=ND, i=DH)
                nc.gpsimd.tensor_tensor(dst, near, far, ALU.mult).then_inc(kv_ok, 1)

            def folds(g, s):
                zz = z[:, s % 2].rearrange("p h c w -> p (h c) w")
                n = g * STEPS + s + 1
                pool.wait_ge(fold1, n)
                nc.gpsimd.tensor_tensor(zz[:, :, 0:16], zz[:, :, 0:16], zz[:, :, 16:32], ALU.add).then_inc(fold2, 1)
                pool.wait_ge(fold2, n)
                nc.gpsimd.tensor_tensor(zz[:, :, 0:8], zz[:, :, 0:8], zz[:, :, 8:16], ALU.add).then_inc(fold3, 1)
                pool.wait_ge(fold3, n)
                if s == 0:
                    after(pool, oT_ps, g * 2)
                dst = o_sb[:, :, s * HS * DH:(s + 1) * HS * DH].rearrange("p c (h j) -> p h c j", h=HS)
                zh = z[:, s % 2]
                nc.gpsimd.tensor_tensor(dst, zh[:, :, :, 0:8], zh[:, :, :, 64:72], ALU.add).then_inc(o_ok, 1)

            def router(n):
                pool.wait_ge(route, n * ROUTE + 2)
                nc.gpsimd.tensor_tensor(lexp[:], euler[:], lsub[:], ALU.pow).then_inc(lexp_ok, 1)
                pool.wait_ge(route, n * ROUTE + 13)
                nc.gpsimd.tensor_tensor(texp[:], euler[:, :, 0], tdif[:], ALU.pow).then_inc(texp_ok, 1)

            def attention(g, n1):
                pairs(g, 0)
                for s in range(STEPS):
                    if s + 1 < STEPS:
                        pairs(g, s + 1)
                    folds(g, s)
                    if s == 2 and n1 is not None:
                        rstd_1(n1)

            nc.gpsimd.memset(half[:], -0.5)
            nc.gpsimd.memset(euler[:], EULER)
            nc.gpsimd.memset(ones[:], 1.0).then_inc(fill_ok, 1)
            pool.wait_ge(fill_ok, 1)
            nc.gpsimd.affine_select(ident[:], ones[:], [[-1, P]], compare_op=ALU.is_equal, fill=0.0,
                                    base=0, channel_multiplier=1).then_inc(consts, 1)
            rstd_1(0)
            nc.gpsimd.memset(z[:], 0.0)
            nc.gpsimd.iota(rank_sb[:], [[0, GB], [-1, E]], base=E, channel_multiplier=0,
                           allow_small_or_imprecise_dtypes=True)
            nc.gpsimd.memset(pick[:], 0.0).then_inc(fill_ok, 1)
            for r in range(2):
                pool.wait_ge(fill_ok, 2 + r)
                nc.gpsimd.affine_select(pick[:], pick[:], [[-1, E], [0, P]], compare_op=ALU.not_equal, fill=1.0,
                                        base=-r * E, channel_multiplier=1).then_inc((fill_ok, consts)[r], 1)
            attention(0, 1)
            rstd_2(0)
            router(0)
            with nc.gpsimd.Fori(1, G - 1) as g:
                attention(g, g + 1)
                rstd_2(g)
                router(g)
            attention(G - 1, None)
            rstd_2(G - 1)
            router(G - 1)


def kernel(x, ctx_2048, L0_xattn_ssm_kernel, L0_xattn_D, L0_ffn_w_gate, L0_ffn_W1, L0_ffn_b1, L0_ffn_W2, L0_ffn_b2):
    import numpy as np
    import concourse.bacc as bacc
    from concourse.bass_utils import run_bass_kernel_spmd as run

    nc = bacc.Bacc("TRN2", target_bir_lowering=False, num_devices=1)
    ssm = np.asarray(L0_xattn_ssm_kernel)
    ahead = np.concatenate([np.zeros((H, P), ssm.dtype), ssm], axis=1)
    arrays = {
        "x": np.asarray(x),
        "ctx": np.asarray(ctx_2048),
        "ssm": np.stack([ahead[:, P - m:P - m + L] for m in range(P)]),
        "d": np.broadcast_to(np.asarray(L0_xattn_D)[None, :], (P, H)),
        "w_gate": np.asarray(L0_ffn_w_gate),
        "w1": np.asarray(L0_ffn_W1),
        "b1t": np.asarray(L0_ffn_b1).T,
        "w2": np.asarray(L0_ffn_W2),
        "b2": np.asarray(L0_ffn_b2),
    }
    arrays = {name: np.ascontiguousarray(a) for name, a in arrays.items()}
    args = [nc.dram_tensor(name, a.shape, mybir.dt.from_np(a.dtype), kind="ExternalInput").ap()
            for name, a in arrays.items()]
    out = nc.dram_tensor("out", (B, HD, L), mybir.dt.float32, kind="ExternalOutput").ap()
    block_kernel(nc, *args, out)
    r = run(nc, [arrays], core_ids=[0])
    return r.results[0]["out"]
```

```python
from contextlib import ExitStack

import concourse.bass as bass
from concourse import mybir

B, HD, L = 16, 128, 256
H, DH = 16, 8
E, I = 8, 128
P = 128
GB = 4
G = B // GB
NC = L // P
CB = NC * GB
TOK = GB * P
ND = DH // 2 + 1
NPAIR = ND * DH
W = DH + ND - 1
HS = 2
STEPS = H // HS
HALF = H // 2
RING = 4
ZW = 72
EPS = 1e-5
EULER = 2.718281828459045


def block_kernel(nc, x, k_src, toep_src, d_src, wgate, w1, b1t, w2, b2, out):
    F32 = mybir.dt.float32
    F32R = mybir.dt.float32r
    ALU = mybir.AluOpType
    ACT = mybir.ActivationFunctionType
    AX = mybir.AxisListType.X

    ctx = ExitStack()
    with ctx:
        def sb(name, shape, dt=F32):
            return ctx.enter_context(nc.sbuf_tensor(name, shape, dt))

        def pb(name):
            return ctx.enter_context(nc.psum_tensor(name, [P, 512], F32))

        def sem(name):
            return ctx.enter_context(nc.semaphore(name))

        toep = sb("toep", [P, H, L])
        w1h = sb("w1h", [P, NC, E, I], F32R)
        w1l = sb("w1l", [P, NC, E, I], F32R)
        w2h = sb("w2h", [P, E, L], F32R)
        w2l = sb("w2l", [P, E, L], F32R)
        wg_sb = sb("wg_sb", [P, NC, E])
        wgh = sb("wgh", [P, NC, E], F32R)
        wgl = sb("wgl", [P, NC, E], F32R)
        b1_sb = sb("b1_sb", [P, E])
        b2_sb = sb("b2_sb", [2 * E, L])
        b2h = sb("b2h", [2 * E, L], F32R)
        b2l = sb("b2l", [2 * E, L], F32R)
        d_sb = sb("d_sb", [P, H])
        ident = sb("ident", [P, P])
        ones = sb("ones", [P, P])
        rank_sb = sb("rank_sb", [P, GB, E])
        half = sb("half", [P, GB])
        euler = sb("euler", [P, GB])
        pick = sb("pick", [2 * E, E, P])
        pickr = sb("pickr", [2 * E, E, P], F32R)
        x_sb = sb("x_sb", [P, B, L])
        xn = sb("xn", [P, GB, L])
        kx = sb("kx", [P, H, NC, GB, W])
        qx = sb("qx", [P, H, NC, GB, W])
        kv = sb("kv", [P, RING, HS, CB * NPAIR])
        z = sb("z", [P, RING, HS, CB, ZW])
        o_sb = sb("o_sb", [P, CB, HD])
        st1 = sb("st1", [P, GB, 6])
        mo1 = sb("mo1", [P, 7, GB])
        rs1 = sb("rs1", [P, GB])
        sh1 = sb("sh1", [P, GB])
        st2 = sb("st2", [P, GB, 6])
        mo2 = sb("mo2", [P, 7, GB])
        rs2 = sb("rs2", [P, GB])
        sh2 = sb("sh2", [P, GB])
        xn2 = sb("xn2", [P, GB, L])
        xh = sb("xh", [P, NC, TOK], F32R)
        xl = sb("xl", [P, NC, TOK], F32R)
        lT = sb("lT", [E, TOK])
        lmax = sb("lmax", [P, GB])
        lsub = sb("lsub", [P, GB, E])
        lexp = sb("lexp", [P, GB, E])
        lsum = sb("lsum", [P, GB])
        lrec = sb("lrec", [P, GB])
        rest = sb("rest", [P, GB, E])
        second = sb("second", [P, GB])
        exp2 = sb("exp2", [P, GB])
        raw2 = sb("raw2", [P, GB])
        eq = sb("eq", [P, GB, E])
        eqr = sb("eqr", [P, GB, E])
        first = sb("first", [P, GB])
        tdif = sb("tdif", [P, GB])
        texp = sb("texp", [P, GB])
        tden = sb("tden", [P, GB])
        tw = sb("tw", [P, GB, 2])
        oh1 = sb("oh1", [P, GB, E])
        oh2 = sb("oh2", [P, GB, E])
        oh1w = sb("oh1w", [P, GB, E])
        oh2w = sb("oh2w", [P, GB, E])
        comb = sb("comb", [P, GB, E])
        combh = sb("combh", [P, GB, E], F32R)
        comb2 = sb("comb2", [P, GB, 2 * E])
        cT = sb("cT", [2 * E, TOK], F32R)
        hg = sb("hg", [P, RING, TOK])
        hw = sb("hw", [P, RING, TOK])
        hh = sb("hh", [P, E, TOK], F32R)
        hl = sb("hl", [P, E, TOK], F32R)
        w1_raw = hw[:].rearrange("p r (e i) -> p (r e) i", i=I).rearrange("p (c e) i -> p c e i", c=NC)
        w2_raw = hg[:].rearrange("p r (e l) -> p (r e) l", l=L)

        y_ps = [pb(f"y_ps{i}") for i in range(2)]
        m1_ps = [pb(f"m1_ps{i}") for i in range(2)]
        ob_ps = [pb(f"ob_ps{i}") for i in range(2)]
        tr_ps = [pb(f"tr_ps{i}") for i in range(2)]

        x0_in = sem("x0_in")
        x_in = sem("x_in")
        kx_in = [sem(f"kx_in{i}") for i in range(2)]
        toep_in = [sem(f"toep_in{i}") for i in range(4)]
        d_in = sem("d_in")
        w_in = sem("w_in")
        stored = sem("stored")
        fill_ok = sem("fill_ok")
        consts = sem("consts")
        toep_mul = sem("toep_mul")
        toep_ok = sem("toep_ok")
        high_ok = sem("high_ok")
        low_ok = sem("low_ok")
        pick_ok = sem("pick_ok")
        moments1 = sem("moments1")
        rstd1 = sem("rstd1")
        shift1 = sem("shift1")
        xn_ok = sem("xn_ok")
        xnT_ps = sem("xnT_ps")
        qx_ok = [sem(f"qx_ok{i}") for i in range(2)]
        kv_ok = sem("kv_ok")
        y_ok = sem("y_ok")
        z_ok = sem("z_ok")
        fold1 = sem("fold1")
        fold2 = sem("fold2")
        fold3 = sem("fold3")
        o_ok = sem("o_ok")
        oT_ps = sem("oT_ps")
        x2_ok = sem("x2_ok")
        moments2 = sem("moments2")
        rstd2 = sem("rstd2")
        shift2 = sem("shift2")
        xn2_ok = sem("xn2_ok")
        x2T_ps = sem("x2T_ps")
        xh_ok = sem("xh_ok")
        xl_ok = sem("xl_ok")
        lT_ps = sem("lT_ps")
        lT_ok = sem("lT_ok")
        logit_ps = sem("logit_ps")
        route = sem("route")
        lexp_ok = sem("lexp_ok")
        exp2_ok = sem("exp2_ok")
        texp_ok = sem("texp_ok")
        cT_ps = sem("cT_ps")
        cT_ok = sem("cT_ok")
        m1_ok = sem("m1_ok")
        gelu_ok = sem("gelu_ok")
        cb_ok = sem("cb_ok")
        hw_ok = sem("hw_ok")
        hh_ok = sem("hh_ok")
        hl_ok = sem("hl_ok")
        m2_ok = sem("m2_ok")
        out_ok = sem("out_ok")
        MOMENTS = 5
        PARTS = 4
        ROUTE_MAX, ROUTE_SECOND, ROUTE_PAIR = 2, 8, 16
        ROUTE = 25

        def after(eng, s, value):
            if not isinstance(value, int) or value > 0:
                eng.wait_ge(s, value)

        def batches(g, first, n):
            return bass.ds(g * GB + first, n)

        toep_rows = H // len(toep_in)
        block = ctx.enter_context(nc.Block())

        @block.sync
        def _(sp):
            def load_k(g, i):
                hs = slice(i * HALF, (i + 1) * HALF)
                src = k_src[bass.ds(g, 1), :, hs].rearrange("g p h n -> p (g h) n")
                sp.dma_start(kx[:, hs].rearrange("p h c b w -> p h (c b w)"), src).then_inc(kx_in[i], 16)

            def next_k(g):
                for i in range(2):
                    sp.wait_ge(kv_ok, g * STEPS + (i + 1) * (STEPS // 2))
                    load_k(g + 1, i)

            def store(n):
                for t in range(GB):
                    sp.wait_ge(out_ok, n * GB + t + 1)
                    sp.dma_start(out[batches(n, t, 1)].rearrange("b p l -> p b l"),
                                 x_sb[:, batches(n, t, 1), :]).then_inc(stored, 16)

            load_k(0, 0)
            sp.dma_start(x_sb[:, 0:GB, :], x[0:GB].rearrange("b p l -> p b l")).then_inc(x0_in, 16)
            sp.dma_start(d_sb[:], d_src).then_inc(d_in, 16)
            for i, s in enumerate(toep_in):
                h0 = i * toep_rows
                sp.dma_start(toep[:, h0:h0 + toep_rows, :], toep_src[:, h0:h0 + toep_rows, :]).then_inc(s, 16)
                if i == 0:
                    load_k(0, 1)
            sp.dma_start(x_sb[:, GB:B, :], x[GB:B].rearrange("b p l -> p b l")).then_inc(x_in, 16)
            for c in range(NC):
                sp.dma_start(w1_raw[:, c], w1[:, c * P:(c + 1) * P].rearrange("e p i -> p e i")).then_inc(w_in, 16)
            sp.dma_start(w2_raw[:], w2.rearrange("e i l -> i e l")).then_inc(w_in, 16)
            sp.dma_start(wg_sb[:], wgate.rearrange("(c p) e -> p c e", p=P)).then_inc(w_in, 16)
            sp.dma_start(b1_sb[:], b1t).then_inc(w_in, 16)
            sp.dma_start(b2_sb[0:E, :], b2).then_inc(w_in, 16)
            sp.dma_start(b2_sb[E:2 * E, :], b2).then_inc(w_in, 16)
            next_k(0)
            with nc.sync.Fori(1, G - 1) as g:
                next_k(g)
                store(g - 1)
            store(G - 2)
            store(G - 1)
            sp.wait_ge(stored, 16 * B)

        WEIGHTS = 7 * 16

        @block.tensor
        def _(pe):
            def product(o, parts, start, stop):
                (ah, al), (bh, bl) = parts
                nc.tensor.matmul(o, ah, bh, start=start, stop=False)
                nc.tensor.matmul(o, ah, bl, start=False, stop=False)
                return nc.tensor.matmul(o, al, bh, start=False, stop=stop)

            def inputs_T(n):
                after(pe, lT_ok, n - 1)
                after(pe, cT_ok, n - 1)
                pe.wait_ge(xn_ok, (n + 1) * GB)
                for c in range(NC):
                    for b in range(GB):
                        t = nc.tensor.transpose(tr_ps[c][:, b * P:(b + 1) * P],
                                                xn[:, b, c * P:(c + 1) * P], ident[:])
                    t.then_inc(xnT_ps, 1)

            def convolve(g, s, first=False):
                pe.wait_ge(kv_ok, g * STEPS + s + 1)
                for hh in range(HS):
                    h = s * HS + hh
                    if first and h % toep_rows == 0:
                        pe.wait_ge(toep_ok, h // toep_rows + 1)
                    after(pe, z_ok, g * H + h - 1)
                    yp, k = y_ps[h % 2], kv[:, s % RING, hh, :]
                    n = GB * NPAIR
                    nc.tensor.matmul(yp[:, 0:2 * n], toep[:, h, 0:P], k, start=True, stop=False)
                    nc.tensor.matmul(yp[:, n:2 * n], toep[:, h, P:2 * P], k[:, 0:n],
                                     start=False, stop=True).then_inc(y_ok, 1)

            def up(n, e):
                if e >= 2:
                    pe.wait_ge(gelu_ok, n * E + e - 1)
                for c in range(NC):
                    t = product(m1_ps[e % 2][:], ((w1h[:, c, e, :], w1l[:, c, e, :]), (xh[:, c, :], xl[:, c, :])),
                                c == 0, c == NC - 1)
                t.then_inc(m1_ok, 1)

            def combine_T(n):
                pe.wait_ge(route, (n + 1) * ROUTE)
                for t in range(GB):
                    last = nc.tensor.transpose(tr_ps[1][0:2 * E, t * P:(t + 1) * P], comb2[:, t, :], ident[:])
                last.then_inc(cT_ps, 1)

            def spread(n, e):
                if e == 0:
                    pe.wait_ge(cT_ok, n + 1)
                elif e >= 2:
                    pe.wait_ge(hw_ok, n * E + e - 1)
                nc.tensor.matmul(ob_ps[e % 2][:], pickr[:, e, :], cT[:], start=True, stop=True).then_inc(cb_ok, 1)

            def down(n, t):
                if t == 0:
                    pe.wait_ge(hh_ok, (n + 1) * E)
                    pe.wait_ge(hl_ok, (n + 1) * E)
                elif t >= 2:
                    pe.wait_ge(out_ok, n * GB + t - 1)
                o = ob_ps[t % 2][:, 0:L]
                tok = slice(t * P, (t + 1) * P)
                for e in range(E):
                    product(o, ((hh[:, e, tok], hl[:, e, tok]), (w2h[:, e, :], w2l[:, e, :])), e == 0, False)
                nc.tensor.matmul(o, cT[:, tok], b2h[:], start=False, stop=False)
                nc.tensor.matmul(o, cT[:, tok], b2l[:], start=False, stop=True).then_inc(m2_ok, 1)

            def attention_T(g, nxt):
                pe.wait_ge(o_ok, (g + 1) * STEPS)
                for p in range(2):
                    if p == 0 and nxt:
                        pe.wait_ge(qx_ok[1], (g + 2) * NC)
                    for bb in range(2):
                        for c in range(NC):
                            t = nc.tensor.transpose(tr_ps[p][:, bb * L + c * P:bb * L + (c + 1) * P],
                                                    o_sb[:, c * GB + 2 * p + bb, :], ident[:])
                    t.then_inc(oT_ps, 1)

            def normed_T(g):
                pe.wait_ge(xn2_ok, (g + 1) * GB)
                for c in range(NC):
                    for b in range(GB):
                        t = nc.tensor.transpose(tr_ps[c][:, b * P:(b + 1) * P],
                                                xn2[:, b, c * P:(c + 1) * P], ident[:])
                    t.then_inc(x2T_ps, 1)

            def logits_T(g):
                pe.wait_ge(xl_ok, (g + 1) * NC)
                for c in range(NC):
                    m = product(tr_ps[0][0:E, :], ((wgh[:, c, :], wgl[:, c, :]), (xh[:, c, :], xl[:, c, :])),
                                c == 0, c == NC - 1)
                m.then_inc(lT_ps, 1)

            def logits(g):
                pe.wait_ge(lT_ok, g + 1)
                for t in range(GB):
                    m = nc.tensor.matmul(tr_ps[1][:, t * E:(t + 1) * E], lT[:, t * P:(t + 1) * P], ident[0:E, 0:E],
                                         start=True, stop=True)
                m.then_inc(logit_ps, 1)

            def up_phase(t, att, exp, nxt):
                n = t - 1
                if att:
                    convolve(t, 4, exp is False)
                if exp:
                    up(n, 0)
                    up(n, 1)
                if att:
                    convolve(t, 5, exp is False)
                if exp:
                    up(n, 2)
                    combine_T(n)
                    spread(n, 0)
                if att:
                    convolve(t, 6, exp is False)
                if exp:
                    up(n, 3)
                    spread(n, 1)
                    up(n, 4)
                    spread(n, 2)
                if att:
                    convolve(t, 7, exp is False)
                if exp:
                    up(n, 5)
                    spread(n, 3)
                    spread(n, 4)
                if nxt:
                    inputs_T(t + 1)
                if exp:
                    up(n, 6)
                    spread(n, 5)
                    up(n, 7)
                    spread(n, 6)
                    spread(n, 7)

            def down_phase(t, tail, exp, nxt):
                n = t - 1
                if nxt:
                    convolve(t + 1, 0, not tail)
                if exp:
                    down(n, 0)
                if tail:
                    attention_T(t, nxt)
                if nxt:
                    convolve(t + 1, 1, not tail)
                if exp:
                    down(n, 1)
                    down(n, 2)
                if tail:
                    normed_T(t)
                if nxt:
                    convolve(t + 1, 2, not tail)
                if tail:
                    if not exp:
                        pe.wait_ge(high_ok, PARTS)
                        pe.wait_ge(low_ok, PARTS)
                        pe.wait_ge(pick_ok, 1)
                    logits_T(t)
                if exp:
                    down(n, 3)
                if tail:
                    logits(t)
                if nxt:
                    convolve(t + 1, 3, not tail)

            pe.wait_ge(consts, 1)
            inputs_T(0)
            down_phase(-1, False, False, True)
            up_phase(0, True, False, True)
            down_phase(0, True, False, True)
            with nc.tensor.Fori(1, G - 1) as t:
                up_phase(t, True, True, True)
                down_phase(t, True, True, True)
            up_phase(G - 1, True, True, False)
            down_phase(G - 1, True, True, False)
            up_phase(G, False, True, False)
            down_phase(G, False, True, False)

        @block.scalar
        def _(act):
            def inputs(n, i):
                after(act, z_ok, (n - 1) * H + (i + 1) * HALF)
                hs = slice(i * HALF, (i + 1) * HALF)
                for c in range(NC):
                    act.wait_ge(xnT_ps, n * NC + c + 1)
                    src = tr_ps[c][:].rearrange("p (b h i) -> p b h i", b=GB, h=H)[:, :, hs, :]
                    d = qx[:, hs, c, :, :].rearrange("p h b w -> p b h w")
                    nc.scalar.copy(d[:, :, :, 0:DH], src)
                    nc.scalar.copy(d[:, :, :, DH:W], src[:, :, :, 0:W - DH]).then_inc(qx_ok[i], 1)

            def norm(g, dst, rs, sh, shift, done):
                act.wait_ge(shift, g + 1)
                for b in range(GB):
                    nc.scalar.activation(dst[:, b, :], x_sb[:, batches(g, b, 1), :].rearrange("p b l -> p (b l)"),
                                         ACT.Identity, bias=sh[:, b:b + 1], scale=rs[:, b:b + 1]).then_inc(done, 1)

            def norm1(n):
                after(act, xnT_ps, n * NC)
                norm(n, xn, rs1, sh1, shift1, xn_ok)

            def normed(g):
                after(act, x2T_ps, g * NC)
                norm(g, xn2, rs2, sh2, shift2, xn2_ok)
                after(act, m1_ok, g * E)
                for c in range(NC):
                    act.wait_ge(x2T_ps, g * NC + c + 1)
                    nc.scalar.copy(xh[:, c, :], tr_ps[c][:]).then_inc(xh_ok, 1)
                act.wait_ge(lT_ps, g + 1)
                nc.scalar.copy(lT[:], tr_ps[0][0:E, :]).then_inc(lT_ok, 1)

            def gelu(n, e):
                act.wait_ge(m1_ok, n * E + e + 1)
                if e >= RING:
                    act.wait_ge(hw_ok, n * E + e - RING + 1)
                nc.scalar.activation(hg[:, e % RING, :], m1_ps[e % 2][:], ACT.Gelu,
                                     bias=b1_sb[:, e:e + 1], scale=1.0).then_inc(gelu_ok, 1)

            def high(n, e):
                act.wait_ge(hw_ok, n * E + e + 1)
                nc.scalar.copy(hh[:, e, :], hw[:, e % RING, :]).then_inc(hh_ok, 1)

            def router(n):
                act.wait_ge(route, n * ROUTE + 2)
                nc.scalar.activation(lexp[:], lsub[:], ACT.Exp).then_inc(lexp_ok, 1)

            def up_phase(t, exp, nxt):
                n = t - 1
                if exp:
                    router(n)
                    gelu(n, 0)
                    gelu(n, 1)
                    gelu(n, 2)
                    gelu(n, 3)
                    high(n, 0)
                if nxt:
                    norm1(t + 1)
                if exp:
                    gelu(n, 4)
                    high(n, 1)
                    high(n, 2)
                    gelu(n, 5)
                    high(n, 3)
                if nxt:
                    inputs(t + 1, 0)
                if exp:
                    high(n, 4)
                    gelu(n, 6)
                    high(n, 5)
                    gelu(n, 7)
                    high(n, 6)
                    high(n, 7)
                if nxt:
                    inputs(t + 1, 1)

            norm1(0)
            inputs(0, 0)
            inputs(0, 1)
            act.wait_ge(w_in, WEIGHTS)
            for dst, src in ((w1h, w1_raw), (w2h, w2_raw), (wgh, wg_sb[:]), (b2h, b2_sb[:])):
                nc.scalar.copy(dst[:], src).then_inc(high_ok, 1)
            up_phase(0, False, True)
            normed(0)
            act.wait_ge(low_ok, PARTS)
            with nc.scalar.Fori(1, G - 1) as t:
                up_phase(t, True, True)
                normed(t)
            up_phase(G - 1, True, False)
            normed(G - 1)
            up_phase(G, True, False)

        @block.vector
        def _(dve):
            def norm(g, st, mo, moments):
                k = [0]

                def step(ins):
                    k[0] += 1
                    ins.then_inc(moments, 1)
                    if k[0] < MOMENTS:
                        dve.wait_ge(moments, g * MOMENTS + k[0])

                for b in range(GB):
                    last = nc.vector.bn_stats(st[:, b, :], x_sb[:, batches(g, b, 1), :].rearrange("p b l -> p (b l)"))
                step(last)
                nc.vector.tensor_tensor(mo[:, 0], st[:, :, 1], st[:, :, 4], ALU.add)
                nc.vector.tensor_tensor(mo[:, 1], st[:, :, 1], st[:, :, 4], ALU.subtract)
                step(nc.vector.tensor_tensor(mo[:, 2], st[:, :, 2], st[:, :, 5], ALU.add))
                nc.vector.tensor_scalar(mo[:, 3], mo[:, 0], -0.5, None, ALU.mult)
                step(nc.vector.scalar_tensor_tensor(mo[:, 4], mo[:, 1], L / 4, mo[:, 1], ALU.mult, ALU.mult))
                step(nc.vector.tensor_tensor(mo[:, 5], mo[:, 4], mo[:, 2], ALU.add))
                step(nc.vector.tensor_scalar(mo[:, 6], mo[:, 5], 1 / L, EPS, ALU.mult, ALU.add))
                assert k[0] == MOMENTS

            def norm1(n):
                norm(n, st1, mo1, moments1)

            def norm2(g):
                norm(g, st2, mo2, moments2)

            def times_q(g, h):
                s, hh_ = h // HS, h % HS
                if h % HALF == 0:
                    dve.wait_ge(qx_ok[h // HALF], (g + 1) * NC)
                if hh_ == 0:
                    after(dve, o_ok, g * STEPS + s - RING + 1)
                dve.wait_ge(y_ok, g * H + h + 1)
                yv = y_ps[h % 2][:, 0:CB * NPAIR].rearrange("p (c d i) -> p c d i", c=CB, d=ND)
                q = qx[:, h, :, :, :].rearrange("p c b w -> p (c b) w")
                q_far = bass.AP(tensor=q.tensor, offset=q.offset, ap=[*q.ap[:2], [1, ND], [1, DH]])
                rows = z[:, s % RING, hh_, :, :]
                nc.vector.tensor_tensor(rows[:, :, 0:NPAIR].rearrange("p c (d i) -> p c d i", d=ND),
                                        yv, q_far, ALU.mult)
                q_near = bass.AP(tensor=q.tensor, offset=q.offset, ap=[*q.ap[:2], [0, ND - 2], [1, DH]])
                lo = NPAIR + 1
                mirror = rows[:, :, lo:lo + (ND - 2) * (DH + 1)].rearrange(
                    "p c (d i) -> p c d i", d=ND - 2)[:, :, :, 0:DH]
                nc.vector.tensor_tensor(mirror, yv[:, :, 1:ND - 1, :], q_near, ALU.mult).then_inc(z_ok, 1)

            def fold(g, s, k):
                if k == 0:
                    dve.wait_ge(z_ok, g * H + (s + 1) * HS)
                else:
                    dve.wait_ge(fold1, g * STEPS + s + 1)
                n = 32 >> k
                zz = z[:, s % RING].rearrange("p h c w -> p (h c) w")
                nc.vector.tensor_tensor(zz[:, :, 0:n], zz[:, :, 0:n], zz[:, :, n:2 * n],
                                        ALU.add).then_inc((fold1, fold2)[k], 1)

            def attend(g, s):
                for k in range(HS):
                    times_q(g, s * HS + k)
                    if s:
                        fold(g, s - 1, k)

            def attend_rest(g):
                for k in range(2):
                    fold(g, STEPS - 1, k)

            def residual(g):
                for p in range(2):
                    dve.wait_ge(oT_ps, g * 2 + p + 1)
                    xs = x_sb[:, batches(g, 2 * p, 2), :]
                    nc.vector.tensor_tensor(xs, xs, tr_ps[p][:].rearrange("p (b l) -> p b l", b=2),
                                            ALU.add).then_inc(x2_ok, 1)

            def stepper(n, done):
                k = [done]

                def step(ins, wait=True):
                    k[0] += 1
                    ins.then_inc(route, 1)
                    if wait:
                        dve.wait_ge(route, n * ROUTE + k[0])
                    return k[0]
                return step

            def wide(ap):
                return bass.AP(tensor=ap.tensor, offset=ap.offset, ap=[*ap.ap[:2], [0, E]])

            def router_max(n):
                step = stepper(n, 0)
                lg = tr_ps[1][:, 0:GB * E].rearrange("p (t e) -> p t e", t=GB)
                dve.wait_ge(logit_ps, n + 1)
                step(nc.vector.reduce_max(lmax[:], lg, AX))
                done = step(nc.vector.tensor_tensor(lsub[:], lg, wide(lmax[:]), ALU.subtract), wait=False)
                assert done == ROUTE_MAX

            def router_top(n):
                step = stepper(n, ROUTE_MAX)

                def first_of(found, oh):
                    step(nc.vector.tensor_tensor(eqr[:], found, rank_sb[:], ALU.mult))
                    step(nc.vector.reduce_max(first[:], eqr[:], AX))
                    step(nc.vector.tensor_tensor(oh, rank_sb[:], wide(first[:]), ALU.is_equal))

                dve.wait_ge(route, n * ROUTE + ROUTE_MAX)
                step(nc.vector.tensor_scalar(eq[:], lsub[:], 0.0, None, ALU.is_equal))
                first_of(eq[:], oh1[:])
                step(nc.vector.scalar_tensor_tensor(rest[:], oh1[:], -3e38, lsub[:], ALU.mult, ALU.add))
                done = step(nc.vector.reduce_max(second[:], rest[:], AX))
                assert done == ROUTE_SECOND
                step(nc.vector.tensor_tensor(eq[:], rest[:], wide(second[:]), ALU.is_equal))
                first_of(eq[:], oh2[:])
                dve.wait_ge(lexp_ok, n + 1)
                step(nc.vector.reduce_sum(lsum[:], lexp[:], AX))
                step(nc.vector.reciprocal(lrec[:], lsum[:]))
                dve.wait_ge(exp2_ok, n + 1)
                step(nc.vector.tensor_tensor(raw2[:], exp2[:], lrec[:], ALU.mult))
                done = step(nc.vector.tensor_tensor(tdif[:], raw2[:], lrec[:], ALU.subtract), wait=False)
                assert done == ROUTE_PAIR

            def router_combine(n):
                step = stepper(n, ROUTE_PAIR)
                dve.wait_ge(texp_ok, n + 1)
                step(nc.vector.tensor_scalar(tden[:], texp[:], 1.0, None, ALU.add))
                step(nc.vector.reciprocal(tw[:, :, 0], tden[:]))
                step(nc.vector.tensor_tensor(tw[:, :, 1], texp[:], tw[:, :, 0], ALU.mult))
                step(nc.vector.tensor_tensor(oh1w[:], oh1[:], wide(tw[:, :, 0]), ALU.mult), wait=False)
                step(nc.vector.tensor_tensor(oh2w[:], oh2[:], wide(tw[:, :, 1]), ALU.mult))
                step(nc.vector.tensor_tensor(comb[:], oh1w[:], oh2w[:], ALU.add))
                step(nc.vector.tensor_copy(combh[:], comb[:]))
                step(nc.vector.tensor_copy(comb2[:, :, 0:E], combh[:].bitcast(F32)), wait=False)
                done = step(nc.vector.tensor_tensor(comb2[:, :, E:2 * E], comb[:], combh[:].bitcast(F32),
                                                    ALU.subtract), wait=False)
                assert done == ROUTE

            def combine(n):
                dve.wait_ge(cT_ps, n + 1)
                nc.vector.tensor_copy(cT[:], tr_ps[1][0:2 * E, :]).then_inc(cT_ok, 1)

            def weigh(n, e):
                dve.wait_ge(gelu_ok, n * E + e + 1)
                dve.wait_ge(cb_ok, n * E + e + 1)
                if e >= RING:
                    dve.wait_ge(hh_ok, n * E + e - RING + 1)
                    dve.wait_ge(hl_ok, n * E + e - RING + 1)
                nc.vector.tensor_tensor(hw[:, e % RING, :], hg[:, e % RING, :], ob_ps[e % 2][:],
                                        ALU.mult).then_inc(hw_ok, 1)

            def lows(g):
                for c in range(NC):
                    dve.wait_ge(xh_ok, g * NC + c + 1)
                    nc.vector.tensor_tensor(xl[:, c, :], tr_ps[c][:], xh[:, c, :].bitcast(F32),
                                            ALU.subtract).then_inc(xl_ok, 1)

            def finish(n, t):
                dve.wait_ge(m2_ok, n * GB + t + 1)
                xs = x_sb[:, batches(n, t, 1), :].rearrange("p b l -> p (b l)")
                nc.vector.tensor_tensor(xs, xs, ob_ps[t % 2][:, 0:L], ALU.add).then_inc(out_ok, 1)

            def up_phase(t, att, exp, nxt):
                n = t - 1
                if exp:
                    router_top(n)
                if att:
                    attend(t, 4)
                if exp:
                    router_combine(n)
                if att:
                    attend(t, 5)
                if exp:
                    combine(n)
                    weigh(n, 0)
                if nxt:
                    norm1(t + 1)
                if att:
                    attend(t, 6)
                if exp:
                    weigh(n, 1)
                    weigh(n, 2)
                if att:
                    attend(t, 7)
                    attend_rest(t)
                if exp:
                    for e in range(3, E):
                        weigh(n, e)

            def down_phase(t, exp, nxt):
                n = t - 1
                if nxt:
                    attend(t + 1, 0)
                residual(t)
                dve.wait_ge(x2_ok, (t + 1) * 2)
                if exp:
                    finish(n, 0)
                norm2(t)
                if nxt:
                    attend(t + 1, 1)
                if exp:
                    finish(n, 1)
                    finish(n, 2)
                lows(t)
                if nxt:
                    attend(t + 1, 2)
                if exp:
                    finish(n, 3)
                router_max(t)
                if nxt:
                    attend(t + 1, 3)

            nc.vector.memset(z[:, :, :, :, NPAIR:ZW], 0.0)
            dve.wait_ge(x0_in, 16)
            norm1(0)
            dve.wait_ge(consts, 1)
            dve.wait_ge(d_in, 16)
            idb = bass.AP(tensor=ident, offset=0, ap=[[P, P], [0, H], [1, P]])
            diag = xn2[:].rearrange("p b l -> p (b l)")
            toep_heads = toep_rows
            for i, s in enumerate(toep_in):
                dwide = bass.AP(tensor=d_sb, offset=i * toep_rows, ap=[[H, P], [1, toep_rows], [0, P]])
                d1 = diag[:, (i % 2) * toep_rows * P:(i % 2 + 1) * toep_rows * P].rearrange("p (h l) -> p h l", l=P)
                idb = bass.AP(tensor=ident, offset=0, ap=[[P, P], [0, toep_rows], [1, P]])
                nc.vector.tensor_tensor(d1, idb, dwide, ALU.mult).then_inc(toep_mul, 1)
                dve.wait_ge(toep_mul, i + 1)
                dve.wait_ge(s, 16)
                hs = slice(i * toep_rows, (i + 1) * toep_rows)
                nc.vector.tensor_tensor(toep[:, hs, 0:P], toep[:, hs, 0:P], d1, ALU.add).then_inc(toep_ok, 1)
            for s in range(STEPS // 2):
                attend(0, s)
            dve.wait_ge(x_in, 16)
            up_phase(0, True, False, True)
            weights = [(w1l, w1_raw, w1h), (w2l, w2_raw, w2h), (wgl, wg_sb[:], wgh), (b2l, b2_sb[:], b2h)]
            for i, (low, full, high) in enumerate(weights):
                dve.wait_ge(high_ok, i + 1)
                nc.vector.tensor_tensor(low[:], full, high[:].bitcast(F32), ALU.subtract).then_inc(low_ok, 1)
            dve.wait_ge(consts, 2)
            nc.vector.tensor_copy(pickr[:], pick[:]).then_inc(pick_ok, 1)
            down_phase(0, False, True)
            with nc.vector.Fori(1, G - 1) as t:
                up_phase(t, True, True, True)
                down_phase(t, True, True)
            up_phase(G - 1, True, True, False)
            down_phase(G - 1, True, False)
            up_phase(G, False, True, False)
            for t in range(GB):
                finish(G - 1, t)

        @block.gpsimd
        def _(pool):
            def rstd(g, mo, rs, sh, moments, rstd_, shift):
                pool.wait_ge(moments, (g + 1) * MOMENTS)
                nc.gpsimd.tensor_tensor(rs[:], mo[:, 6], half[:], ALU.pow).then_inc(rstd_, 1)
                pool.wait_ge(rstd_, g + 1)
                nc.gpsimd.tensor_tensor(sh[:], mo[:, 3], rs[:], ALU.mult).then_inc(shift, 1)

            def rstd_1(n):
                rstd(n, mo1, rs1, sh1, moments1, rstd1, shift1)

            def rstd_2(g):
                rstd(g, mo2, rs2, sh2, moments2, rstd2, shift2)

            def pairs(g, s):
                if s % (STEPS // 2) == 0:
                    pool.wait_ge(kx_in[s * HS // HALF], (g + 1) * 16)
                after(pool, y_ok, g * H + (s - RING + 1) * HS)
                k = kx[:, s * HS:(s + 1) * HS].rearrange("p h c b w -> p (h c b) w")
                near = bass.AP(tensor=k.tensor, offset=k.offset, ap=[*k.ap[:2], [0, ND], [1, DH]])
                far = bass.AP(tensor=k.tensor, offset=k.offset, ap=[*k.ap[:2], [1, ND], [1, DH]])
                dst = kv[:, s % RING].rearrange("p h (c d i) -> p (h c) d i", d=ND, i=DH)
                nc.gpsimd.tensor_tensor(dst, near, far, ALU.mult).then_inc(kv_ok, 1)

            def folds(g, s):
                zz = z[:, s % RING].rearrange("p h c w -> p (h c) w")
                n = g * STEPS + s + 1
                pool.wait_ge(fold2, n)
                nc.gpsimd.tensor_tensor(zz[:, :, 0:8], zz[:, :, 0:8], zz[:, :, 8:16], ALU.add).then_inc(fold3, 1)
                pool.wait_ge(fold3, n)
                if s == 0:
                    after(pool, oT_ps, g * 2)
                dst = o_sb[:, :, s * HS * DH:(s + 1) * HS * DH].rearrange("p c (h j) -> p h c j", h=HS)
                zh = z[:, s % RING]
                nc.gpsimd.tensor_tensor(dst, zh[:, :, :, 0:8], zh[:, :, :, 64:72], ALU.add).then_inc(o_ok, 1)

            def low(n, e):
                pool.wait_ge(hh_ok, n * E + e + 1)
                nc.gpsimd.tensor_tensor(hl[:, e, :], hw[:, e % RING, :], hh[:, e, :].bitcast(F32),
                                        ALU.subtract).then_inc(hl_ok, 1)

            def second_exp(n):
                pool.wait_ge(route, n * ROUTE + ROUTE_SECOND)
                nc.gpsimd.tensor_tensor(exp2[:], euler[:], second[:], ALU.pow).then_inc(exp2_ok, 1)

            def pair_exp(n):
                pool.wait_ge(route, n * ROUTE + ROUTE_PAIR)
                nc.gpsimd.tensor_tensor(texp[:], euler[:], tdif[:], ALU.pow).then_inc(texp_ok, 1)

            def up_phase(t, att, exp, nxt):
                n = t - 1
                if exp:
                    second_exp(n)
                if att:
                    pairs(t, 6)
                if exp:
                    pair_exp(n)
                if att:
                    folds(t, 3)
                    pairs(t, 7)
                    folds(t, 4)
                if nxt:
                    rstd_1(t + 1)
                if exp:
                    low(n, 0)
                if att:
                    folds(t, 5)
                if nxt:
                    pairs(t + 1, 0)
                if exp:
                    low(n, 1)
                    low(n, 2)
                if att:
                    folds(t, 6)
                    folds(t, 7)
                if nxt:
                    pairs(t + 1, 1)
                if exp:
                    for e in range(3, E):
                        low(n, e)

            def down_phase(t, tail, nxt):
                if nxt:
                    pairs(t + 1, 2)
                if tail:
                    rstd_2(t)
                if nxt:
                    pairs(t + 1, 3)
                    folds(t + 1, 0)
                    pairs(t + 1, 4)
                    folds(t + 1, 1)
                    pairs(t + 1, 5)
                    folds(t + 1, 2)

            nc.gpsimd.memset(half[:], -0.5)
            nc.gpsimd.memset(euler[:], EULER)
            nc.gpsimd.memset(ones[:], 1.0).then_inc(fill_ok, 1)
            pool.wait_ge(fill_ok, 1)
            nc.gpsimd.affine_select(ident[:], ones[:], [[-1, P]], compare_op=ALU.is_equal, fill=0.0,
                                    base=0, channel_multiplier=1).then_inc(consts, 1)
            rstd_1(0)
            for s in range(2):
                pairs(0, s)
            nc.gpsimd.iota(rank_sb[:], [[0, GB], [-1, E]], base=E, channel_multiplier=0,
                           allow_small_or_imprecise_dtypes=True)
            nc.gpsimd.memset(pick[:], 0.0).then_inc(fill_ok, 1)
            for r in range(2):
                pool.wait_ge(fill_ok, 2 + r)
                nc.gpsimd.affine_select(pick[:], pick[:], [[-1, E], [0, P]], compare_op=ALU.not_equal, fill=1.0,
                                        base=-r * E, channel_multiplier=1).then_inc((fill_ok, consts)[r], 1)
            down_phase(-1, False, True)
            up_phase(0, True, False, True)
            down_phase(0, True, True)
            with nc.gpsimd.Fori(1, G - 1) as t:
                up_phase(t, True, True, True)
                down_phase(t, True, True)
            up_phase(G - 1, True, True, False)
            down_phase(G - 1, True, False)
            up_phase(G, False, True, False)


def kernel(x, ctx_2048, L0_xattn_ssm_kernel, L0_xattn_D, L0_ffn_w_gate, L0_ffn_W1, L0_ffn_b1, L0_ffn_W2, L0_ffn_b2):
    import numpy as np
    import concourse.bacc as bacc
    from concourse.bass_utils import run_bass_kernel_spmd as run

    nc = bacc.Bacc("TRN2", target_bir_lowering=False, num_devices=1)
    ssm = np.asarray(L0_xattn_ssm_kernel)
    k = np.asarray(ctx_2048).reshape(G, GB, H, DH, NC, P).transpose(0, 5, 2, 4, 1, 3)
    ahead = np.concatenate([np.zeros((H, P), ssm.dtype), ssm], axis=1)
    arrays = {
        "x": np.asarray(x),
        "k": np.concatenate([k, k[..., :W - DH]], axis=-1).reshape(G, P, H, CB * W),
        "ssm": np.stack([ahead[:, P - m:P - m + L] for m in range(P)]),
        "d": np.broadcast_to(np.asarray(L0_xattn_D)[None, :], (P, H)),
        "w_gate": np.asarray(L0_ffn_w_gate),
        "w1": np.asarray(L0_ffn_W1),
        "b1t": np.asarray(L0_ffn_b1).T,
        "w2": np.asarray(L0_ffn_W2),
        "b2": np.asarray(L0_ffn_b2),
    }
    arrays = {name: np.ascontiguousarray(a) for name, a in arrays.items()}
    args = [nc.dram_tensor(name, a.shape, mybir.dt.from_np(a.dtype), kind="ExternalInput").ap()
            for name, a in arrays.items()]
    out = nc.dram_tensor("out", (B, HD, L), mybir.dt.float32, kind="ExternalOutput").ap()
    block_kernel(nc, *args, out)
    r = run(nc, [arrays], core_ids=[0])
    return r.results[0]["out"]
```

```python
from contextlib import ExitStack

import concourse.bass as bass
from concourse import mybir

B, HD, L = 16, 128, 256
H, DH = 16, 8
E, I = 8, 128
P = 128
GB = 4
G = B // GB
NC = L // P
CB = NC * GB
TOK = GB * P
ND = DH // 2 + 1
NPAIR = ND * DH
W = DH + ND - 1
HS = 2
STEPS = H // HS
HALF = H // 2
RING = 4
ZW = 72
CR = P // 2
EPS = 1e-5
EULER = 2.718281828459045


def block_kernel(nc, x, k_src, toep_src, d_src, wgate, w1, b1t, w2, b2, out):
    F32 = mybir.dt.float32
    F32R = mybir.dt.float32r
    ALU = mybir.AluOpType
    ACT = mybir.ActivationFunctionType
    AX = mybir.AxisListType.X

    ctx = ExitStack()
    with ctx:
        def sb(name, shape, dt=F32):
            return ctx.enter_context(nc.sbuf_tensor(name, shape, dt))

        def pb(name):
            return ctx.enter_context(nc.psum_tensor(name, [P, 512], F32))

        def sem(name):
            return ctx.enter_context(nc.semaphore(name))

        toep = sb("toep", [P, H, L])
        w1h = sb("w1h", [P, NC, E, I], F32R)
        w1l = sb("w1l", [P, NC, E, I], F32R)
        w2h = sb("w2h", [P, E, L], F32R)
        w2l = sb("w2l", [P, E, L], F32R)
        wg_sb = sb("wg_sb", [P, NC, E])
        wgh = sb("wgh", [P, NC, E], F32R)
        wgl = sb("wgl", [P, NC, E], F32R)
        b1_sb = sb("b1_sb", [P, E])
        b2_sb = sb("b2_sb", [CR, L])
        b2r = sb("b2r", [CR, L], F32R)
        d_sb = sb("d_sb", [P, H])
        ident = sb("ident", [P, P])
        ones = sb("ones", [P, P])
        rank_sb = sb("rank_sb", [P, GB, E])
        half = sb("half", [P, GB])
        euler = sb("euler", [P, GB])
        pick = sb("pick", [2 * E, E, P])
        pickr = sb("pickr", [2 * E, E, P], F32R)
        x_sb = sb("x_sb", [P, B, L])
        xn = sb("xn", [P, GB, L])
        kx = sb("kx", [P, H, NC, GB, W])
        qx = sb("qx", [P, H, NC, GB, W])
        kv = sb("kv", [P, RING, HS, CB * NPAIR])
        z = sb("z", [P, RING, HS, CB, ZW])
        o_sb = sb("o_sb", [P, CB, HD])
        st1 = sb("st1", [P, GB, 6])
        mo1 = sb("mo1", [P, 7, GB])
        rs1 = sb("rs1", [P, GB])
        sh1 = sb("sh1", [P, GB])
        st2 = sb("st2", [P, GB, 6])
        mo2 = sb("mo2", [P, 7, GB])
        rs2 = sb("rs2", [P, GB])
        sh2 = sb("sh2", [P, GB])
        xn2 = sb("xn2", [P, GB, L])
        xh = sb("xh", [P, NC, TOK], F32R)
        xl = sb("xl", [P, NC, TOK], F32R)
        lT = sb("lT", [E, TOK])
        lmax = sb("lmax", [P, GB])
        lsub = sb("lsub", [P, GB, E])
        lexp = sb("lexp", [P, GB, E])
        lsum = sb("lsum", [P, GB])
        lrec = sb("lrec", [P, GB])
        rest = sb("rest", [P, GB, E])
        second = sb("second", [P, GB])
        exp2 = sb("exp2", [P, GB])
        raw2 = sb("raw2", [P, GB])
        eq = sb("eq", [P, GB, E])
        eqr = sb("eqr", [P, GB, E])
        first = sb("first", [P, GB])
        tdif = sb("tdif", [P, GB])
        texp = sb("texp", [P, GB])
        tden = sb("tden", [P, GB])
        tw = sb("tw", [P, GB, 2])
        oh1 = sb("oh1", [P, GB, E])
        oh2 = sb("oh2", [P, GB, E])
        oh1w = sb("oh1w", [P, GB, E])
        oh2w = sb("oh2w", [P, GB, E])
        comb = sb("comb", [P, GB, E])
        combh = sb("combh", [P, GB, E], F32R)
        comb2 = sb("comb2", [P, GB, 4, P // 4])
        cT = sb("cT", [CR, TOK], F32R)
        hg = sb("hg", [P, RING, TOK])
        hw = sb("hw", [P, RING, TOK])
        hh = sb("hh", [P, E, TOK], F32R)
        hl = sb("hl", [P, E, TOK], F32R)
        diag = hg[:].rearrange("p r (q l) -> p (r q) l", l=P)
        w1_raw = hw[:].rearrange("p r (e i) -> p (r e) i", i=I).rearrange("p (c e) i -> p c e i", c=NC)
        w2_raw = hg[:].rearrange("p r (e l) -> p (r e) l", l=L)

        y_ps = [pb(f"y_ps{i}") for i in range(2)]
        m1_ps = [pb(f"m1_ps{i}") for i in range(2)]
        ob_ps = [pb(f"ob_ps{i}") for i in range(2)]
        tr_ps = [pb(f"tr_ps{i}") for i in range(2)]

        down_ps = m1_ps + ob_ps
        last_ps = y_ps + tr_ps

        x0_in = sem("x0_in")
        x1_in = sem("x1_in")
        x_in = sem("x_in")
        kx_in = [sem(f"kx_in{i}") for i in range(2)]
        toep_in = [sem(f"toep_in{i}") for i in range(4)]
        d_in = sem("d_in")
        w_in = sem("w_in")
        stored = sem("stored")
        fill_ok = sem("fill_ok")
        consts = sem("consts")
        diag_ok = sem("diag_ok")
        toep_ok = sem("toep_ok")
        high_ok = sem("high_ok")
        low_ok = sem("low_ok")
        w1l_ok = sem("w1l_ok")
        pick_ok = sem("pick_ok")
        moments1 = sem("moments1")
        rstd1 = sem("rstd1")
        shift1 = sem("shift1")
        xn_ok = sem("xn_ok")
        xnT_ps = sem("xnT_ps")
        qx_ok = [sem(f"qx_ok{i}") for i in range(2)]
        kv_ok = sem("kv_ok")
        y_ok = sem("y_ok")
        z_ok = sem("z_ok")
        fold1 = sem("fold1")
        fold2 = sem("fold2")
        fold3 = sem("fold3")
        o_ok = sem("o_ok")
        oT_ps = sem("oT_ps")
        x2_ok = sem("x2_ok")
        moments2 = sem("moments2")
        rstd2 = sem("rstd2")
        shift2 = sem("shift2")
        xn2_ok = sem("xn2_ok")
        x2T_ps = sem("x2T_ps")
        xh_ok = sem("xh_ok")
        xl_ok = sem("xl_ok")
        lT_ps = sem("lT_ps")
        lT_ok = sem("lT_ok")
        logit_ps = sem("logit_ps")
        route = sem("route")
        lexp_ok = sem("lexp_ok")
        exp2_ok = sem("exp2_ok")
        texp_ok = sem("texp_ok")
        cT_ps = sem("cT_ps")
        cT_ok = sem("cT_ok")
        m1_ok = sem("m1_ok")
        gelu_ok = sem("gelu_ok")
        cb_ok = sem("cb_ok")
        hw_ok = sem("hw_ok")
        hh_ok = sem("hh_ok")
        hl_ok = sem("hl_ok")
        hl2_ok = sem("hl2_ok")
        m2_ok = sem("m2_ok")
        out_ok = sem("out_ok")
        MOMENTS = 5
        PARTS = 4
        LOW_POOL = 4
        ROUTE_MAX, ROUTE_SECOND, ROUTE_PAIR = 2, 8, 14
        ROUTE = 24

        def after(eng, s, value):
            if not isinstance(value, int) or value > 0:
                eng.wait_ge(s, value)

        def batches(g, first, n):
            return bass.ds(g * GB + first, n)

        toep_rows = H // len(toep_in)
        block = ctx.enter_context(nc.Block())

        @block.sync
        def _(sp):
            def load_k(g, i):
                hs = slice(i * HALF, (i + 1) * HALF)
                src = k_src[bass.ds(g, 1), :, hs].rearrange("g p h n -> p (g h) n")
                sp.dma_start(kx[:, hs].rearrange("p h c b w -> p h (c b w)"), src).then_inc(kx_in[i], 16)

            def next_k(g):
                for i in range(2):
                    sp.wait_ge(kv_ok, g * STEPS + (i + 1) * (STEPS // 2))
                    load_k(g + 1, i)

            def store(n):
                for t in range(GB):
                    sp.wait_ge(out_ok, n * GB + t + 1)
                    sp.dma_start(out[batches(n, t, 1)].rearrange("b p l -> p b l"),
                                 x_sb[:, batches(n, t, 1), :]).then_inc(stored, 16)

            sp.dma_start(d_sb[:], d_src).then_inc(d_in, 16)
            load_k(0, 0)
            for i, s in enumerate(toep_in):
                h0 = i * toep_rows
                sp.dma_start(toep[:, h0:h0 + toep_rows, :], toep_src[:, h0:h0 + toep_rows, :]).then_inc(s, 16)
                if i == 0:
                    sp.dma_start(x_sb[:, GB:2 * GB, :], x[GB:2 * GB].rearrange("b p l -> p b l")).then_inc(x1_in, 16)
            load_k(0, 1)
            sp.dma_start(x_sb[:, 2 * GB:B, :], x[2 * GB:B].rearrange("b p l -> p b l")).then_inc(x_in, 16)
            for c in range(NC):
                sp.dma_start(w1_raw[:, c], w1[:, c * P:(c + 1) * P].rearrange("e p i -> p e i")).then_inc(w_in, 16)
            sp.wait_ge(toep_ok, len(toep_in))
            sp.dma_start(w2_raw[:], w2.rearrange("e i l -> i e l")).then_inc(w_in, 16)
            sp.dma_start(wg_sb[:], wgate.rearrange("(c p) e -> p c e", p=P)).then_inc(w_in, 16)
            sp.dma_start(b1_sb[:], b1t).then_inc(w_in, 16)
            sp.dma_start(b2_sb[:], b2).then_inc(w_in, 16)
            next_k(0)
            with nc.sync.Fori(1, G - 1) as g:
                next_k(g)
                store(g - 1)
            store(G - 2)
            store(G - 1)
            sp.wait_ge(stored, 16 * B)

        WEIGHTS = 6 * 16

        @block.tensor
        def _(pe):
            def product(o, parts, start, stop):
                (ah, al), (bh, bl) = parts
                nc.tensor.matmul(o, ah, bh, start=start, stop=False)
                nc.tensor.matmul(o, ah, bl, start=False, stop=False)
                return nc.tensor.matmul(o, al, bh, start=False, stop=stop)

            def inputs_T(n):
                after(pe, lT_ok, n - 1)
                after(pe, cT_ok, n - 1)
                for b in range(GB):
                    pe.wait_ge(xn_ok, n * GB + b + 1)
                    for c in range(NC):
                        t = nc.tensor.transpose(tr_ps[c][:, b * P:(b + 1) * P],
                                                xn[:, b, c * P:(c + 1) * P], ident[:])
                        if b == GB - 1:
                            t.then_inc(xnT_ps, 1)

            def convolve(g, s, first=False):
                pe.wait_ge(kv_ok, g * STEPS + s + 1)
                for hh in range(HS):
                    h = s * HS + hh
                    if first and h % toep_rows == 0:
                        pe.wait_ge(toep_ok, h // toep_rows + 1)
                    after(pe, z_ok, g * H + h - 1)
                    yp, k = y_ps[h % 2], kv[:, s % RING, hh, :]
                    n = GB * NPAIR
                    nc.tensor.matmul(yp[:, 0:2 * n], toep[:, h, 0:P], k, start=True, stop=False)
                    nc.tensor.matmul(yp[:, n:2 * n], toep[:, h, P:2 * P], k[:, 0:n],
                                     start=False, stop=True).then_inc(y_ok, 1)

            def up(n, e):
                if e >= 2:
                    pe.wait_ge(gelu_ok, n * E + e - 1)
                else:
                    after(pe, out_ok, (n - 1) * GB + e + 1)
                for c in range(NC):
                    t = product(m1_ps[e % 2][:], ((w1h[:, c, e, :], w1l[:, c, e, :]), (xh[:, c, :], xl[:, c, :])),
                                c == 0, c == NC - 1)
                t.then_inc(m1_ok, 1)

            def combine_T(n):
                pe.wait_ge(route, (n + 1) * ROUTE)
                for t in range(GB):
                    last = nc.tensor.transpose(tr_ps[1][:, t * P:(t + 1) * P],
                                               comb2[:, t].rearrange("p a r -> p (a r)"), ident[:])
                last.then_inc(cT_ps, 1)

            def spread(n, e):
                if e == 0:
                    pe.wait_ge(cT_ok, n + 1)
                if e >= 2:
                    pe.wait_ge(hw_ok, n * E + e - 1)
                else:
                    after(pe, out_ok, n * GB + e - 1)
                nc.tensor.matmul(ob_ps[e % 2][:], pickr[:, e, :], cT[0:2 * E, :],
                                 start=True, stop=True).then_inc(cb_ok, 1)

            def outputs(n, t, experts, last=False):
                if experts[0] == 0:
                    if last:
                        if t == 0:
                            pe.wait_ge(z_ok, (n + 1) * H)
                    elif t < 2:
                        pe.wait_ge(gelu_ok, n * E + 7 + t)
                    else:
                        pe.wait_ge(hw_ok, n * E + 5 + t)
                o = (last_ps if last else down_ps)[t][:, 0:L]
                tok = slice(t * P, (t + 1) * P)
                for e in experts:
                    if t == 0 and e < LOW_POOL:
                        pe.wait_ge(hl_ok, n * LOW_POOL + e + 1)
                    elif t == 0:
                        pe.wait_ge(hl2_ok, n * (E - LOW_POOL) + e - LOW_POOL + 1)
                    product(o, ((hh[:, e, tok], hl[:, e, tok]), (w2h[:, e, :], w2l[:, e, :])), e == 0, False)
                if experts[-1] == E - 1:
                    nc.tensor.matmul(o, cT[:, tok], b2r[:], start=False, stop=True).then_inc(m2_ok, 1)

            def down(n, experts, last=False):
                for t in range(GB):
                    outputs(n, t, experts, last)

            def attention_T(g, nxt):
                pe.wait_ge(o_ok, (g + 1) * STEPS)
                for p in range(2):
                    if p == 0 and nxt:
                        pe.wait_ge(qx_ok[1], (g + 2) * NC)
                    for bb in range(2):
                        for c in range(NC):
                            t = nc.tensor.transpose(tr_ps[p][:, bb * L + c * P:bb * L + (c + 1) * P],
                                                    o_sb[:, c * GB + 2 * p + bb, :], ident[:])
                    t.then_inc(oT_ps, 1)

            def normed_T(g):
                for b in range(GB):
                    pe.wait_ge(xn2_ok, g * GB + b + 1)
                    for c in range(NC):
                        t = nc.tensor.transpose(tr_ps[c][:, b * P:(b + 1) * P],
                                                xn2[:, b, c * P:(c + 1) * P], ident[:])
                        if b == GB - 1:
                            t.then_inc(x2T_ps, 1)

            def logits_T(g):
                pe.wait_ge(xl_ok, (g + 1) * NC)
                for c in range(NC):
                    m = product(tr_ps[0][0:E, :], ((wgh[:, c, :], wgl[:, c, :]), (xh[:, c, :], xl[:, c, :])),
                                c == 0, c == NC - 1)
                m.then_inc(lT_ps, 1)

            def logits(g):
                pe.wait_ge(lT_ok, g + 1)
                for t in range(GB):
                    m = nc.tensor.matmul(tr_ps[1][:, t * E:(t + 1) * E], lT[:, t * P:(t + 1) * P], ident[0:E, 0:E],
                                         start=True, stop=True)
                m.then_inc(logit_ps, 1)

            def iteration(t, prev, tail, nxt):
                n = t - 1
                if prev:
                    spread(n, 2)
                    up(n, 4)
                if tail:
                    convolve(t, 6, not prev)
                if prev:
                    spread(n, 3)
                    up(n, 5)
                if tail:
                    convolve(t, 7, not prev)
                if prev:
                    spread(n, 4)
                    up(n, 6)
                    spread(n, 5)
                    up(n, 7)
                if nxt:
                    inputs_T(t + 1)
                    convolve(t + 1, 0, not tail)
                if tail:
                    attention_T(t, nxt)
                if prev:
                    spread(n, 6)
                    spread(n, 7)
                if nxt:
                    convolve(t + 1, 1, not tail)
                if prev:
                    down(n, range(LOW_POOL))
                if tail:
                    normed_T(t)
                if nxt:
                    convolve(t + 1, 2, not tail)
                if prev:
                    outputs(n, 0, range(LOW_POOL, E))
                if tail:
                    if not prev:
                        pe.wait_ge(high_ok, PARTS)
                        pe.wait_ge(low_ok, 1)
                    logits_T(t)
                if nxt:
                    convolve(t + 1, 3, not tail)
                if prev and not nxt:
                    outputs(n, 1, range(LOW_POOL, E))
                if tail:
                    logits(t)
                if prev:
                    for tile in range(1 if nxt else 2, GB):
                        outputs(n, tile, range(LOW_POOL, E))
                if nxt:
                    convolve(t + 1, 4, not tail)
                if tail:
                    if not prev:
                        pe.wait_ge(w1l_ok, 1)
                    up(t, 0)
                    up(t, 1)
                    up(t, 2)
                    combine_T(t)
                    up(t, 3)
                    if not prev:
                        pe.wait_ge(low_ok, PARTS - 1)
                        pe.wait_ge(pick_ok, 1)
                    spread(t, 0)
                    spread(t, 1)
                if nxt:
                    convolve(t + 1, 5, not tail)

            def last_group(n):
                for e in range(4, E):
                    up(n, e)
                    if e == 4:
                        spread(n, 2)
                    spread(n, e - 1)
                    if e % 2:
                        down(n, range(e // 2 - 2, e // 2 - 1), True)
                spread(n, E - 1)
                down(n, range(2, E), True)

            pe.wait_ge(consts, 1)
            iteration(-1, False, False, True)
            iteration(0, False, True, True)
            with nc.tensor.Fori(1, G - 1) as t:
                iteration(t, True, True, True)
            iteration(G - 1, True, True, False)
            last_group(G - 1)

        @block.scalar
        def _(act):
            def inputs(n, i):
                after(act, z_ok, (n - 1) * H + (i + 1) * HALF)
                hs = slice(i * HALF, (i + 1) * HALF)
                for c in range(NC):
                    act.wait_ge(xnT_ps, n * NC + c + 1)
                    src = tr_ps[c][:].rearrange("p (b h i) -> p b h i", b=GB, h=H)[:, :, hs, :]
                    d = qx[:, hs, c, :, :].rearrange("p h b w -> p b h w")
                    nc.scalar.copy(d[:, :, :, 0:DH], src)
                    nc.scalar.copy(d[:, :, :, DH:W], src[:, :, :, 0:W - DH]).then_inc(qx_ok[i], 1)

            def norm(g, dst, rs, sh, shift, done):
                act.wait_ge(shift, g + 1)
                for b in range(GB):
                    nc.scalar.activation(dst[:, b, :], x_sb[:, batches(g, b, 1), :].rearrange("p b l -> p (b l)"),
                                         ACT.Identity, bias=sh[:, b:b + 1], scale=rs[:, b:b + 1]).then_inc(done, 1)

            def norm1(n):
                after(act, xnT_ps, n * NC)
                norm(n, xn, rs1, sh1, shift1, xn_ok)

            def normed(g):
                after(act, x2T_ps, g * NC)
                norm(g, xn2, rs2, sh2, shift2, xn2_ok)
                after(act, m1_ok, g * E)
                for c in range(NC):
                    act.wait_ge(x2T_ps, g * NC + c + 1)
                    nc.scalar.copy(xh[:, c, :], tr_ps[c][:]).then_inc(xh_ok, 1)
                act.wait_ge(lT_ps, g + 1)
                nc.scalar.copy(lT[:], tr_ps[0][0:E, :]).then_inc(lT_ok, 1)

            def gelu(n, e):
                act.wait_ge(m1_ok, n * E + e + 1)
                if e >= RING:
                    act.wait_ge(hw_ok, n * E + e - RING + 1)
                nc.scalar.activation(hg[:, e % RING, :], m1_ps[e % 2][:], ACT.Gelu,
                                     bias=b1_sb[:, e:e + 1], scale=1.0).then_inc(gelu_ok, 1)

            def high(n, e):
                act.wait_ge(hw_ok, n * E + e + 1)
                nc.scalar.copy(hh[:, e, :], hw[:, e % RING, :]).then_inc(hh_ok, 1)

            def combine(n):
                act.wait_ge(cT_ps, n + 1)
                nc.scalar.copy(cT[:], tr_ps[1][0:CR, :]).then_inc(cT_ok, 1)

            def router(n):
                act.wait_ge(route, n * ROUTE + ROUTE_MAX)
                nc.scalar.activation(lexp[:], lsub[:], ACT.Exp).then_inc(lexp_ok, 1)

            def iteration(t, prev, tail, nxt):
                n = t - 1
                if prev:
                    gelu(n, 4)
                    gelu(n, 5)
                    high(n, 2)
                    if nxt:
                        norm1(t + 1)
                    high(n, 3)
                if nxt:
                    inputs(t + 1, 0)
                    inputs(t + 1, 1)
                if prev:
                    gelu(n, 6)
                    gelu(n, 7)
                    for e in range(4, E):
                        high(n, e)
                if tail:
                    normed(t)
                    if not prev:
                        act.wait_ge(low_ok, PARTS - 1)
                    router(t)
                    gelu(t, 0)
                    gelu(t, 1)
                    combine(t)
                    gelu(t, 2)
                    high(t, 0)
                    gelu(t, 3)
                    high(t, 1)

            nc.scalar.dma_start(x_sb[:, 0:GB, :], x[0:GB].rearrange("b p l -> p b l")).then_inc(x0_in, 16)
            norm1(0)
            inputs(0, 0)
            inputs(0, 1)
            norm1(1)
            act.wait_ge(w_in, WEIGHTS)
            for dst, src in ((wgh, wg_sb[:]), (w1h, w1_raw), (w2h, w2_raw), (b2r, b2_sb[:])):
                nc.scalar.copy(dst[:], src).then_inc(high_ok, 1)
            iteration(0, False, True, True)
            with nc.scalar.Fori(1, G - 1) as t:
                iteration(t, True, True, True)
            iteration(G - 1, True, True, False)
            for e in range(4, E):
                gelu(G - 1, e)
                high(G - 1, e - 2)
            high(G - 1, E - 2)
            high(G - 1, E - 1)

        @block.vector
        def _(dve):
            def norm(g, st, mo, moments):
                k = [0]

                def step(ins):
                    k[0] += 1
                    ins.then_inc(moments, 1)
                    if k[0] < MOMENTS:
                        dve.wait_ge(moments, g * MOMENTS + k[0])

                for b in range(GB):
                    last = nc.vector.bn_stats(st[:, b, :], x_sb[:, batches(g, b, 1), :].rearrange("p b l -> p (b l)"))
                step(last)
                nc.vector.tensor_tensor(mo[:, 0], st[:, :, 1], st[:, :, 4], ALU.add)
                nc.vector.tensor_tensor(mo[:, 1], st[:, :, 1], st[:, :, 4], ALU.subtract)
                step(nc.vector.tensor_tensor(mo[:, 2], st[:, :, 2], st[:, :, 5], ALU.add))
                nc.vector.tensor_scalar(mo[:, 3], mo[:, 0], -0.5, None, ALU.mult)
                step(nc.vector.scalar_tensor_tensor(mo[:, 4], mo[:, 1], L / 4, mo[:, 1], ALU.mult, ALU.mult))
                step(nc.vector.tensor_tensor(mo[:, 5], mo[:, 4], mo[:, 2], ALU.add))
                step(nc.vector.tensor_scalar(mo[:, 6], mo[:, 5], 1 / L, EPS, ALU.mult, ALU.add))
                assert k[0] == MOMENTS

            def norm1(n):
                norm(n, st1, mo1, moments1)

            def norm2(g):
                norm(g, st2, mo2, moments2)

            def times_q(g, h):
                s, hh_ = h // HS, h % HS
                if h % HALF == 0:
                    dve.wait_ge(qx_ok[h // HALF], (g + 1) * NC)
                if hh_ == 0:
                    after(dve, o_ok, g * STEPS + s - RING + 1)
                dve.wait_ge(y_ok, g * H + h + 1)
                yv = y_ps[h % 2][:, 0:CB * NPAIR].rearrange("p (c d i) -> p c d i", c=CB, d=ND)
                q = qx[:, h, :, :, :].rearrange("p c b w -> p (c b) w")
                q_far = bass.AP(tensor=q.tensor, offset=q.offset, ap=[*q.ap[:2], [1, ND], [1, DH]])
                rows = z[:, s % RING, hh_, :, :]
                nc.vector.tensor_tensor(rows[:, :, 0:NPAIR].rearrange("p c (d i) -> p c d i", d=ND),
                                        yv, q_far, ALU.mult)
                q_near = bass.AP(tensor=q.tensor, offset=q.offset, ap=[*q.ap[:2], [0, ND - 2], [1, DH]])
                lo = NPAIR + 1
                mirror = rows[:, :, lo:lo + (ND - 2) * (DH + 1)].rearrange(
                    "p c (d i) -> p c d i", d=ND - 2)[:, :, :, 0:DH]
                nc.vector.tensor_tensor(mirror, yv[:, :, 1:ND - 1, :], q_near, ALU.mult).then_inc(z_ok, 1)

            def fold(g, s, k):
                if k == 0:
                    dve.wait_ge(z_ok, g * H + (s + 1) * HS)
                else:
                    dve.wait_ge(fold1, g * STEPS + s + 1)
                n = 32 >> k
                zz = z[:, s % RING].rearrange("p h c w -> p (h c) w")
                nc.vector.tensor_tensor(zz[:, :, 0:n], zz[:, :, 0:n], zz[:, :, n:2 * n],
                                        ALU.add).then_inc((fold1, fold2)[k], 1)

            def attend(g, s):
                for k in range(HS):
                    times_q(g, s * HS + k)
                    if s:
                        fold(g, s - 1, k)

            def attend_rest(g):
                for k in range(2):
                    fold(g, STEPS - 1, k)

            def residual(g):
                for p in range(2):
                    dve.wait_ge(oT_ps, g * 2 + p + 1)
                    xs = x_sb[:, batches(g, 2 * p, 2), :]
                    nc.vector.tensor_tensor(xs, xs, tr_ps[p][:].rearrange("p (b l) -> p b l", b=2),
                                            ALU.add).then_inc(x2_ok, 1)

            def stepper(n, done):
                k = [done]

                def step(ins, wait=True):
                    k[0] += 1
                    ins.then_inc(route, 1)
                    if wait:
                        dve.wait_ge(route, n * ROUTE + k[0])
                    return k[0]
                return step

            def twice(ap):
                return bass.AP(tensor=ap.tensor, offset=ap.offset, ap=[*ap.ap[:2], [0, 2], ap.ap[2]])

            def wide(ap):
                return bass.AP(tensor=ap.tensor, offset=ap.offset, ap=[*ap.ap[:2], [0, E]])

            def router_max(n):
                step = stepper(n, 0)
                lg = tr_ps[1][:, 0:GB * E].rearrange("p (t e) -> p t e", t=GB)
                dve.wait_ge(logit_ps, n + 1)
                step(nc.vector.reduce_max(lmax[:], lg, AX))
                done = step(nc.vector.tensor_tensor(lsub[:], lg, wide(lmax[:]), ALU.subtract), wait=False)
                assert done == ROUTE_MAX

            def router_top(n):
                step = stepper(n, ROUTE_MAX)

                def first_of(oh):
                    step(nc.vector.tensor_tensor(oh, rank_sb[:], wide(first[:]), ALU.is_equal))

                dve.wait_ge(route, n * ROUTE + ROUTE_MAX)
                step(nc.vector.scalar_tensor_tensor(eqr[:], lsub[:], 0.0, rank_sb[:], ALU.is_equal, ALU.mult))
                step(nc.vector.reduce_max(first[:], eqr[:], AX))
                first_of(oh1[:])
                step(nc.vector.scalar_tensor_tensor(rest[:], oh1[:], -3e38, lsub[:], ALU.mult, ALU.add), wait=False)
                dve.wait_ge(lexp_ok, n + 1)
                step(nc.vector.reduce_sum(lsum[:], lexp[:], AX))
                done = step(nc.vector.reduce_max(second[:], rest[:], AX), wait=False)
                assert done == ROUTE_SECOND
                step(nc.vector.reciprocal(lrec[:], lsum[:]))
                step(nc.vector.tensor_tensor(eq[:], rest[:], wide(second[:]), ALU.is_equal))
                step(nc.vector.tensor_tensor(eqr[:], eq[:], rank_sb[:], ALU.mult))
                step(nc.vector.reduce_max(first[:], eqr[:], AX))
                dve.wait_ge(exp2_ok, n + 1)
                step(nc.vector.tensor_tensor(raw2[:], exp2[:], lrec[:], ALU.mult))
                done = step(nc.vector.tensor_tensor(tdif[:], raw2[:], lrec[:], ALU.subtract), wait=False)
                assert done == ROUTE_PAIR
                first_of(oh2[:])

            def router_combine(n):
                step = stepper(n, ROUTE_PAIR + 1)
                dve.wait_ge(texp_ok, n + 1)
                step(nc.vector.tensor_scalar(tden[:], texp[:], 1.0, None, ALU.add))
                step(nc.vector.reciprocal(tw[:, :, 0], tden[:]))
                step(nc.vector.tensor_tensor(tw[:, :, 1], texp[:], tw[:, :, 0], ALU.mult), wait=False)
                step(nc.vector.tensor_tensor(oh1w[:], oh1[:], wide(tw[:, :, 0]), ALU.mult))
                step(nc.vector.tensor_tensor(oh2w[:], oh2[:], wide(tw[:, :, 1]), ALU.mult))
                step(nc.vector.tensor_tensor(comb[:], oh1w[:], oh2w[:], ALU.add))
                step(nc.vector.tensor_copy(combh[:], comb[:]))
                high = twice(combh[:].bitcast(F32))
                step(nc.vector.tensor_copy(comb2[:, :, 0:2, 0:E], high), wait=False)
                done = step(nc.vector.tensor_tensor(comb2[:, :, 0:2, E:2 * E], twice(comb[:]), high, ALU.subtract),
                            wait=False)
                assert done == ROUTE

            def weigh(n, e, first=False):
                dve.wait_ge(gelu_ok, n * E + e + 1)
                dve.wait_ge(cb_ok, n * E + e + 1)
                if first:
                    dve.wait_ge(w1l_ok, 1)
                if e >= RING:
                    dve.wait_ge(hh_ok, n * E + e - RING + 1)
                    dve.wait_ge(hl_ok, n * LOW_POOL + e - RING + 1)
                nc.vector.tensor_tensor(hw[:, e % RING, :], hg[:, e % RING, :], ob_ps[e % 2][:],
                                        ALU.mult).then_inc(hw_ok, 1)

            def low(n, e):
                dve.wait_ge(hh_ok, n * E + e + 1)
                nc.vector.tensor_tensor(hl[:, e, :], hw[:, e % RING, :], hh[:, e, :].bitcast(F32),
                                        ALU.subtract).then_inc(hl2_ok, 1)

            def weight_low(part, full, high, highs):
                dve.wait_ge(high_ok, highs)
                nc.vector.tensor_tensor(part, full, high.bitcast(F32), ALU.subtract).then_inc(low_ok, 1)

            def add_diagonal(i):
                dve.wait_ge(diag_ok, i + 1)
                dve.wait_ge(toep_in[i], 16)
                hs = slice(i * toep_rows, (i + 1) * toep_rows)
                nc.vector.tensor_tensor(toep[:, hs, 0:P], toep[:, hs, 0:P], diag[:, hs], ALU.add).then_inc(toep_ok, 1)

            def lows(g):
                for c in range(NC):
                    dve.wait_ge(xh_ok, g * NC + c + 1)
                    nc.vector.tensor_tensor(xl[:, c, :], tr_ps[c][:], xh[:, c, :].bitcast(F32),
                                            ALU.subtract).then_inc(xl_ok, 1)

            def finish(n, t, last=False):
                dve.wait_ge(m2_ok, n * GB + t + 1)
                xs = x_sb[:, batches(n, t, 1), :].rearrange("p b l -> p (b l)")
                nc.vector.tensor_tensor(xs, xs, (last_ps if last else down_ps)[t][:, 0:L], ALU.add).then_inc(out_ok, 1)

            def iteration(t, prev, tail, nxt):
                n = t - 1
                if tail:
                    if prev and nxt:
                        norm1(t + 1)
                    attend(t, 6)
                if prev:
                    weigh(n, 2)
                    weigh(n, 3)
                if tail:
                    attend(t, 7)
                    attend_rest(t)
                if prev:
                    weigh(n, 4)
                    weigh(n, 5)
                if nxt:
                    attend(t + 1, 0)
                    if not tail:
                        add_diagonal(3)
                if tail:
                    residual(t)
                    dve.wait_ge(x2_ok, (t + 1) * 2)
                if prev:
                    weigh(n, 6)
                if tail:
                    norm2(t)
                if prev:
                    weigh(n, 7)
                if nxt:
                    attend(t + 1, 1)
                if prev:
                    for e in range(LOW_POOL, E):
                        low(n, e)
                elif tail:
                    weight_low(wgl[:], wg_sb[:], wgh[:], 1)
                    weight_low(w2l[:], w2_raw, w2h[:], 3)
                if tail:
                    lows(t)
                if tail and not prev:
                    weight_low(b2r[CR // 2:], b2_sb[CR // 2:], b2r[CR // 2:], 4)
                if nxt:
                    attend(t + 1, 2)
                    attend(t + 1, 3)
                if prev:
                    finish(n, 0)
                if tail:
                    router_max(t)
                    router_top(t)
                if prev:
                    finish(n, 1)
                    finish(n, 2)
                if tail:
                    router_combine(t)
                if prev:
                    finish(n, 3)
                if nxt:
                    attend(t + 1, 4)
                if tail:
                    weigh(t, 0, first=not prev)
                if nxt:
                    attend(t + 1, 5)
                if tail:
                    weigh(t, 1)

            nc.vector.memset(z[:, :, :, :, NPAIR:ZW], 0.0)
            nc.vector.memset(comb2[:], 0.0)
            dve.wait_ge(x0_in, 16)
            norm1(0)
            add_diagonal(0)
            dve.wait_ge(consts, 2)
            nc.vector.tensor_copy(pickr[:], pick[:]).then_inc(pick_ok, 1)
            dve.wait_ge(x1_in, 16)
            dve.wait_ge(shift1, 1)
            norm1(1)
            add_diagonal(1)
            add_diagonal(2)
            iteration(-1, False, False, True)
            iteration(0, False, True, True)
            dve.wait_ge(x_in, 16)
            with nc.vector.Fori(1, G - 1) as t:
                iteration(t, True, True, True)
            iteration(G - 1, True, True, False)
            for e in range(2, E):
                weigh(G - 1, e)
                if e > LOW_POOL:
                    low(G - 1, e - 1)
            low(G - 1, E - 1)
            for t in range(GB):
                finish(G - 1, t, True)

        @block.gpsimd
        def _(pool):
            def rstd(g, mo, rs, sh, moments, rstd_, shift):
                pool.wait_ge(moments, (g + 1) * MOMENTS)
                nc.gpsimd.tensor_tensor(rs[:], mo[:, 6], half[:], ALU.pow).then_inc(rstd_, 1)
                pool.wait_ge(rstd_, g + 1)
                nc.gpsimd.tensor_tensor(sh[:], mo[:, 3], rs[:], ALU.mult).then_inc(shift, 1)

            def rstd_1(n):
                rstd(n, mo1, rs1, sh1, moments1, rstd1, shift1)

            def rstd_2(g):
                rstd(g, mo2, rs2, sh2, moments2, rstd2, shift2)

            def pairs(g, s):
                if s % (STEPS // 2) == 0:
                    pool.wait_ge(kx_in[s * HS // HALF], (g + 1) * 16)
                after(pool, y_ok, g * H + (s - RING + 1) * HS)
                k = kx[:, s * HS:(s + 1) * HS].rearrange("p h c b w -> p (h c b) w")
                near = bass.AP(tensor=k.tensor, offset=k.offset, ap=[*k.ap[:2], [0, ND], [1, DH]])
                far = bass.AP(tensor=k.tensor, offset=k.offset, ap=[*k.ap[:2], [1, ND], [1, DH]])
                dst = kv[:, s % RING].rearrange("p h (c d i) -> p (h c) d i", d=ND, i=DH)
                nc.gpsimd.tensor_tensor(dst, near, far, ALU.mult).then_inc(kv_ok, 1)

            def folds(g, s):
                zz = z[:, s % RING].rearrange("p h c w -> p (h c) w")
                n = g * STEPS + s + 1
                pool.wait_ge(fold2, n)
                nc.gpsimd.tensor_tensor(zz[:, :, 0:8], zz[:, :, 0:8], zz[:, :, 8:16], ALU.add).then_inc(fold3, 1)
                pool.wait_ge(fold3, n)
                if s == 0:
                    after(pool, oT_ps, g * 2)
                dst = o_sb[:, :, s * HS * DH:(s + 1) * HS * DH].rearrange("p c (h j) -> p h c j", h=HS)
                zh = z[:, s % RING]
                nc.gpsimd.tensor_tensor(dst, zh[:, :, :, 0:8], zh[:, :, :, 64:72], ALU.add).then_inc(o_ok, 1)

            def low(n, e):
                pool.wait_ge(hh_ok, n * E + e + 1)
                nc.gpsimd.tensor_tensor(hl[:, e, :], hw[:, e % RING, :], hh[:, e, :].bitcast(F32),
                                        ALU.subtract).then_inc(hl_ok, 1)

            def second_exp(n):
                pool.wait_ge(route, n * ROUTE + ROUTE_SECOND)
                nc.gpsimd.tensor_tensor(exp2[:], euler[:], second[:], ALU.pow).then_inc(exp2_ok, 1)

            def pair_exp(n):
                pool.wait_ge(route, n * ROUTE + ROUTE_PAIR)
                nc.gpsimd.tensor_tensor(texp[:], euler[:], tdif[:], ALU.pow).then_inc(texp_ok, 1)

            def iteration(t, prev, tail, nxt):
                n = t - 1
                if tail and nxt:
                    if prev:
                        rstd_1(t + 1)
                    pairs(t + 1, 0)
                if prev:
                    low(n, 0)
                    low(n, 1)
                if tail:
                    folds(t, 5)
                    folds(t, 6)
                    folds(t, 7)
                    if nxt:
                        pairs(t + 1, 1)
                if prev:
                    for e in range(2, LOW_POOL):
                        low(n, e)
                if nxt:
                    pairs(t + 1, 2)
                if tail:
                    rstd_2(t)
                if nxt:
                    pairs(t + 1, 3)
                    folds(t + 1, 0)
                    pairs(t + 1, 4)
                if tail and not prev:
                    pool.wait_ge(high_ok, 2)
                    nc.gpsimd.tensor_tensor(w1l[:], w1_raw, w1h[:].bitcast(F32), ALU.subtract).then_inc(w1l_ok, 1)
                if nxt:
                    folds(t + 1, 1)
                    pairs(t + 1, 5)
                if tail:
                    second_exp(t)
                    pair_exp(t)
                if nxt:
                    folds(t + 1, 2)
                    pairs(t + 1, 6)
                    folds(t + 1, 3)
                    pairs(t + 1, 7)
                    folds(t + 1, 4)

            nc.gpsimd.memset(half[:], -0.5)
            nc.gpsimd.memset(euler[:], EULER)
            nc.gpsimd.memset(ones[:], 1.0).then_inc(fill_ok, 1)
            pool.wait_ge(fill_ok, 1)
            nc.gpsimd.affine_select(ident[:], ones[:], [[-1, P]], compare_op=ALU.is_equal, fill=0.0,
                                    base=0, channel_multiplier=1).then_inc(consts, 1)
            nc.gpsimd.memset(pick[:], 0.0).then_inc(fill_ok, 1)
            pool.wait_ge(d_in, 16)
            for i in range(len(toep_in)):
                d_wide = bass.AP(tensor=d_sb, offset=i * toep_rows, ap=[[H, P], [1, toep_rows], [0, P]])
                nc.gpsimd.affine_select(diag[:, i * toep_rows:(i + 1) * toep_rows], d_wide, [[0, toep_rows], [-1, P]],
                                        compare_op=ALU.is_equal, fill=0.0, base=0,
                                        channel_multiplier=1).then_inc(diag_ok, 1)
            for r in range(2):
                pool.wait_ge(fill_ok, 2 + r)
                nc.gpsimd.affine_select(pick[:], pick[:], [[-1, E], [0, P]], compare_op=ALU.not_equal, fill=1.0,
                                        base=-r * E, channel_multiplier=1).then_inc((fill_ok, consts)[r], 1)
            rstd_1(0)
            pairs(0, 0)
            pairs(0, 1)
            nc.gpsimd.iota(rank_sb[:], [[0, GB], [-1, E]], base=E, channel_multiplier=0,
                           allow_small_or_imprecise_dtypes=True)
            pool.wait_ge(xn_ok, GB)
            rstd_1(1)
            iteration(-1, False, False, True)
            iteration(0, False, True, True)
            with nc.gpsimd.Fori(1, G - 1) as t:
                iteration(t, True, True, True)
            iteration(G - 1, True, True, False)
            iteration(G, True, False, False)


def kernel(x, ctx_2048, L0_xattn_ssm_kernel, L0_xattn_D, L0_ffn_w_gate, L0_ffn_W1, L0_ffn_b1, L0_ffn_W2, L0_ffn_b2):
    import numpy as np
    import concourse.bacc as bacc
    from concourse.bass_utils import run_bass_kernel_spmd as run

    nc = bacc.Bacc("TRN2", target_bir_lowering=False, num_devices=1)
    ssm = np.asarray(L0_xattn_ssm_kernel)
    k = np.asarray(ctx_2048).reshape(G, GB, H, DH, NC, P).transpose(0, 5, 2, 4, 1, 3)
    ahead = np.concatenate([np.zeros((H, P), ssm.dtype), ssm], axis=1)
    arrays = {
        "x": np.asarray(x),
        "k": np.concatenate([k, k[..., :W - DH]], axis=-1).reshape(G, P, H, CB * W),
        "ssm": np.stack([ahead[:, P - m:P - m + L] for m in range(P)]),
        "d": np.broadcast_to(np.asarray(L0_xattn_D)[None, :], (P, H)),
        "w_gate": np.asarray(L0_ffn_w_gate),
        "w1": np.asarray(L0_ffn_W1),
        "b1t": np.asarray(L0_ffn_b1).T,
        "w2": np.asarray(L0_ffn_W2),
        "b2": np.tile(np.asarray(L0_ffn_b2), (CR // E, 1)),
    }
    arrays = {name: np.ascontiguousarray(a) for name, a in arrays.items()}
    args = [nc.dram_tensor(name, a.shape, mybir.dt.from_np(a.dtype), kind="ExternalInput").ap()
            for name, a in arrays.items()]
    out = nc.dram_tensor("out", (B, HD, L), mybir.dt.float32, kind="ExternalOutput").ap()
    block_kernel(nc, *args, out)
    r = run(nc, [arrays], core_ids=[0])
    return r.results[0]["out"]
```
